# Optimizing a Trainium2 kernel written in Bass

```python
import numpy as np
import jax
import jax.numpy as jnp

def _softmax(x, axis=-1):
    return jax.nn.softmax(x, axis=axis)

def _gelu(x):
    return jax.nn.gelu(x, approximate=True)

def _silu(x):
    return jax.nn.silu(x)

def _sigmoid(x):
    return jax.nn.sigmoid(x)

def _layernorm(x, axis=-1, eps=1e-05):
    m = jnp.mean(x, axis=axis, keepdims=True)
    v = jnp.var(x, axis=axis, keepdims=True)
    return (x - m) / jnp.sqrt(v + eps)

def _scatter_add(tgt, idx, src, axis=0):
    return tgt.at[idx].add(src)

def _segment_sum(src, seg, n):
    return jax.ops.segment_sum(src, seg, n)
kernel_name = 'mk_xattn_ffn_d1_seqx_r8_4145a1'

def setup_inputs(seed: int=0):
    np.random.seed(seed)
    _w = jnp.asarray

    def _rec_inputs():
        import jax
        import jax.numpy as jnp
        _rk = jax.random.key(seed)
        x = 0.5 + 0.2887 * jax.random.normal(jax.random.fold_in(_rk, 1), (4, 256, 256), jnp.float32)
        _lenS = 256 - jax.random.randint(jax.random.fold_in(_rk, 7), (4,), 0, max(1, 256 // 4) + 1, jnp.int32)
        _lenS2 = 256 - jax.random.randint(jax.random.fold_in(_rk, 8), (4,), 0, max(1, 256 // 4) + 1, jnp.int32)
        _ctx_512P = jax.random.normal(jax.random.fold_in(_rk, 11), (4, 16, 64), jnp.float32)
        _ctx_512c = jax.random.dirichlet(jax.random.fold_in(_rk, 511), 0.3 * jnp.ones((16,), jnp.float32), (4, 256))
        _ctx_512t = jnp.einsum('bsk,bkd->bsd', _ctx_512c, _ctx_512P)
        _ctx_512t = _ctx_512t * jax.lax.rsqrt(jnp.mean(jnp.square(_ctx_512t)) + 1e-12) * 0.953939
        ctx_512 = -0.000392918 + 0.999932 * (_ctx_512t + 0.3 * jax.random.normal(jax.random.fold_in(_rk, 611), (4, 256, 64), jnp.float32))
        return (x, ctx_512)
    x, ctx_512 = _rec_inputs()

    def _L0_xattn_setup():
        import jax, jax.numpy as jnp
        import numpy as np
        B, N, D = (16, 256, 64)
        H = 4
        TOP_K_RATIO = 0.3
        key = jax.random.key(seed)
        k1, k2, k3, k4 = jax.random.split(key, 4)
        h = jax.random.normal(k1, (B, N, D), dtype=jnp.float32)
        adj_raw = jax.random.uniform(k2, (B, N, N), dtype=jnp.float32)
        lim = 1.0 / np.sqrt(D)
        Wq = jax.random.uniform(k3, (D, D), minval=-lim, maxval=lim, dtype=jnp.float32)
        Wk = jax.random.uniform(k4, (D, D), minval=-lim, maxval=lim, dtype=jnp.float32)
        gamma_raw = jnp.float32(-0.85)
        return {'h': h, 'adj_raw': adj_raw, 'Wq': Wq, 'Wk': Wk, 'gamma_raw': gamma_raw}
    _L0_xattn_all = _L0_xattn_setup()
    _L0_xattn_in = {k: v for k, v in _L0_xattn_all.items() if k in ('Wq', 'Wk', 'gamma_raw')}
    del _L0_xattn_all

    def _L0_ffn_setup():
        import jax, jax.numpy as jnp
        import numpy as np
        B, S, H = (1, 64, 256)
        I = 192
        E = 32
        K = 4
        SCALE = 1.8
        key = jax.random.key(seed)
        ks = jax.random.split(key, 9)
        init = lambda k, shape: jax.random.normal(k, shape, jnp.float32) * (1.0 / np.sqrt(shape[-1]))
        return {'x': jax.random.normal(ks[0], (B, S, H), jnp.float32), 'router_w': init(ks[1], (E, H)), 'router_b': jnp.zeros((E,), jnp.float32), 'gate_w': init(ks[2], (E, I, H)), 'up_w': init(ks[3], (E, I, H)), 'down_w': init(ks[4], (E, H, I)), 'shared_gate_w': init(ks[5], (I, H)), 'shared_up_w': init(ks[6], (I, H)), 'shared_down_w': init(ks[7], (H, I))}
    _L0_ffn_all = _L0_ffn_setup()
    _L0_ffn_in = {k: v for k, v in _L0_ffn_all.items() if k in ('router_w', 'router_b', 'gate_w', 'up_w', 'down_w', 'shared_gate_w', 'shared_up_w', 'shared_down_w')}
    del _L0_ffn_all
    return {'x': x, 'ctx_512': ctx_512, 'L0_xattn_Wq': _L0_xattn_in['Wq'], 'L0_xattn_Wk': _L0_xattn_in['Wk'], 'L0_xattn_gamma_raw': _L0_xattn_in['gamma_raw'], 'L0_ffn_router_w': _L0_ffn_in['router_w'], 'L0_ffn_router_b': _L0_ffn_in['router_b'], 'L0_ffn_gate_w': _L0_ffn_in['gate_w'], 'L0_ffn_up_w': _L0_ffn_in['up_w'], 'L0_ffn_down_w': _L0_ffn_in['down_w'], 'L0_ffn_shared_gate_w': _L0_ffn_in['shared_gate_w'], 'L0_ffn_shared_up_w': _L0_ffn_in['shared_up_w'], 'L0_ffn_shared_down_w': _L0_ffn_in['shared_down_w']}

def reference(x, ctx_512, L0_xattn_Wq, L0_xattn_Wk, L0_xattn_gamma_raw, L0_ffn_router_w, L0_ffn_router_b, L0_ffn_gate_w, L0_ffn_up_w, L0_ffn_down_w, L0_ffn_shared_gate_w, L0_ffn_shared_up_w, L0_ffn_shared_down_w):
    import jax
    import jax.numpy as jnp

    def _L0_xattn_ref(h, adj_raw, Wq, Wk, gamma_raw):
        import jax, jax.numpy as jnp
        import numpy as np
        B, N, D = (16, 256, 64)
        H = 4
        TOP_K_RATIO = 0.3
        b, n, dm = h.shape
        d = dm // H
        Q = (h @ Wq.T).reshape(b, n, H, d).transpose(0, 2, 1, 3)
        K = (h @ Wk.T).reshape(b, n, H, d).transpose(0, 2, 1, 3)
        sim = jnp.einsum('bhnd,bhmd->bnm', Q, K) / (jnp.sqrt(jnp.float32(d)) * H)
        k = max(1, int(n * TOP_K_RATIO))
        topk_vals = jax.lax.top_k(sim, k)[0]
        threshold = topk_vals[:, :, -1:]
        sparse_mask = (sim >= threshold).astype(sim.dtype)
        A_learned = jax.nn.sigmoid(sim) * sparse_mask
        A_learned = (A_learned + jnp.swapaxes(A_learned, -1, -2)) * 0.5
        gamma = jax.nn.sigmoid(gamma_raw)
        return (1.0 - gamma) * adj_raw + gamma * A_learned

    def _L0_ffn_ref(x, router_w, router_b, gate_w, up_w, down_w, shared_gate_w, shared_up_w, shared_down_w):
        import jax, jax.numpy as jnp
        import numpy as np
        B, S, H = (1, 64, 256)
        I = 192
        E = 32
        K = 4
        SCALE = 1.8
        b, s, h = x.shape
        xf = x.reshape(-1, h).astype(jnp.float32)
        logits = xf @ router_w.T + router_b
        top_vals, top_idx = jax.lax.top_k(logits, K)
        rw = jax.nn.softmax(top_vals, axis=-1) * SCALE
        combine = jnp.einsum('tke,tk->te', jax.nn.one_hot(top_idx, E, dtype=xf.dtype), rw)
        g = jax.nn.silu(jnp.einsum('th,eih->tei', xf, gate_w))
        u = jnp.einsum('th,eih->tei', xf, up_w)
        routed = jnp.einsum('tei,ehi,te->th', g * u, down_w, combine)
        sg = jax.nn.silu(xf @ shared_gate_w.T)
        su = xf @ shared_up_w.T
        shared = sg * su @ shared_down_w.T
        return (routed + shared).reshape(b, s, h)
    x = x + _L0_xattn_ref(ctx_512, _layernorm(x, axis=-1), L0_xattn_Wq, L0_xattn_Wk, L0_xattn_gamma_raw)
    x = x + _L0_ffn_ref(_layernorm(x, axis=-1), L0_ffn_router_w, L0_ffn_router_b, L0_ffn_gate_w, L0_ffn_up_w, L0_ffn_down_w, L0_ffn_shared_gate_w, L0_ffn_shared_up_w, L0_ffn_shared_down_w)
    return x

_drawn_inputs = setup_inputs


def setup_inputs(seed=0):
    import zlib

    import numpy as np

    out = dict(_drawn_inputs(seed))
    spreads = {'L0_ffn_router_b': (0.0, 0.1)}
    factors = {}
    for name, (base, spread) in spreads.items():
        noise = np.random.default_rng([zlib.crc32(name.encode()), seed]).standard_normal(out[name].shape)
        drawn = base * np.exp(spread * noise) if base else spread * noise
        out[name] = jnp.asarray(drawn.astype(out[name].dtype))
    for name, factor in factors.items():
        out[name] = (out[name] * factor).astype(out[name].dtype)
    return out
```

```python
import concourse.bass as bass
from concourse import mybir
from contextlib import ExitStack

P = 128
NB, N, H, DC = 4, 256, 256, 64
TOK = NB * N
NJ = TOK // P
E, I, TOPK = 32, 192, 4
KTH = int(N * 0.3)
EPS = 1e-5
ROUTE_SCALE = 1.8
SIM_SCALE = 1.0 / 16.0
KH = H // P
IC = I // 2
GU = 2 * I
XW = H + E
MAX_TILES = E + (TOK * TOPK - E) // P
UNROLL = 4
LEAD = 3
GROUPS = -(-MAX_TILES // UNROLL)
NCOL = 72
assert NCOL >= GROUPS * UNROLL + 2 + LEAD and NCOL % 4 == 0
ROWS = TOK + P
NEG = -3.0e38
WGRP = 4


def build(nc, x, ctx_t, wqk, gamma, router_w, router_b, w_gu, w_down, ws_gu, ws_down, out):
    f32, f16 = mybir.dt.float32, mybir.dt.float16
    i32, u32 = mybir.dt.int32, mybir.dt.uint32
    ALU = mybir.AluOpType
    ACT = mybir.ActivationFunctionType
    AX = mybir.AxisListType.X

    rows_dram = nc.dram_tensor("token_rows", (ROWS, XW), f32, kind="Internal").ap()
    acc_dram = [nc.dram_tensor(f"acc{a}", (ROWS, H), f32, kind="Internal").ap() for a in range(2)]

    ctx = ExitStack()
    with ctx:
        def sb(name, shape, dt=f32):
            return ctx.enter_context(nc.sbuf_tensor(name, shape, dt))

        def sem(name):
            return ctx.enter_context(nc.semaphore(name))

        wgu_sb = sb("wgu_sb", [P, E, KH * GU])
        wd_sb = sb("wd_sb", [IC, E, 2 * H])
        wsgu_sb = sb("wsgu_sb", [P, KH * GU])
        wsd_sb = sb("wsd_sb", [IC, 2 * H])
        rw_sb = sb("rw_sb", [P, KH * E])
        rb_sb = sb("rb_sb", [P, E])
        x_sb = sb("x_sb", [P, NJ, H])
        xg_sb = x_sb[:, 0:5, :].rearrange("p j h -> p (j h)")[:, 0:4 * XW].rearrange("p (u w) -> p u w", u=4)
        arena = sb("arena", [P, 4864])
        ctx_sb = arena[0:DC, 0:1024]
        qt_sb = arena[0:DC, 1024:2048]
        kt_sb = arena[0:DC, 2048:3072]
        s_sb = arena[:, 3072:3584].rearrange("p (i n) -> p i n", i=2)
        sig_sb = arena[:, 3584:4096].rearrange("p (i n) -> p i n", i=2)
        a_sb = arena[:, 4096:4608].rearrange("p (i n) -> p i n", i=2)
        onehot = arena[:, 0:512].bitcast(f16).rearrange("p (c e) -> p c e", e=E)
        prod = arena[:, 512:1536].rearrange("p (c e) -> p c e", e=E)
        slot_oh = arena[:, 1536:3584].bitcast(f16).rearrange("p (c s) -> p c s", s=P)
        tile_oh = arena[:, 3584:3584 + 16 * NCOL].bitcast(f16).rearrange("p (c t) -> p c t", t=NCOL)
        work_sb = sb("work_sb", [P, 2, N])
        wqk_sb = sb("wqk_sb", [DC, 2 * DC])
        xn_sb = sb("xn_sb", [P, 2, H])
        xt_sb = sb("xt_sb", [P, 2, KH * P])
        sg_sb = sb("sg_sb", [P, 2, I])
        h_sb = sb("h_sb", [P, 2, I])
        iota_i = h_sb[:, 0, 0:P].bitcast(i32)
        ht_sb = sb("ht_sb", [IC, 2, 2 * P])
        y_sb = sb("y_sb", [P, 2, H])
        gu_cp = sb("gu_cp", [P, GU])
        ident = sb("ident", [P, P])
        zero_sb = sb("zero_sb", [P, XW])
        ones_f = sb("ones_f", [P, E])
        ones_h = sb("ones_h", [P, P], f16)
        before_h = sb("before_h", [P, P], f16)
        iota_f = sb("iota_f", [P, P])
        iota_h = sb("iota_h", [P, P], f16)
        pidx_i = sb("pidx_i", [P, NJ], i32)
        tok1 = sb("tok1", [P, NJ])
        pad_row = sb("pad_row", [P, 1])
        pidx = sb("pidx", [P, 1])
        gam = sb("gam", [P, 4])
        st1 = sb("st1", [P, NJ, 6])
        mv1 = sb("mv1", [P, NJ, 2])
        r1 = sb("r1", [P, 6, NJ])
        half = sb("half", [P, 1])
        st2 = sb("st2", [P, 2, 6])
        mv2 = sb("mv2", [P, 2, 2])
        r2 = sb("r2", [P, 5, 2])
        m8 = sb("m8", [P, 2, 8])
        lg_sb = sb("lg_sb", [P, 2, E])
        v8 = sb("v8", [P, NJ, 8])
        i8 = sb("i8", [P, NJ, 8], u32)
        idx_f = sb("idx_f", [P, NJ, TOPK])
        ex = sb("ex", [P, NJ, TOPK])
        sm = sb("sm", [P, 3, NJ])
        rw = sb("rw", [P, NJ, TOPK])
        comb = sb("comb", [P, NJ, E])
        cnt_i = sb("cnt_i", [P, 2, E], i32)
        ntl = work_sb[:, 0, 0:4 * E].rearrange("p (n e) -> p n e", e=E)
        srank = work_sb[:, 1, :].rearrange("p (j e) -> p j e", e=E)
        sl_f = sb("sl_f", [P, NJ * TOPK])
        sl_i = work_sb[:, 0, 4 * E:4 * E + 3 * NJ * TOPK].bitcast(i32).rearrange("p (n c) -> p n c", n=3)
        sl_p = sb("sl_p", [P, 2, NJ * TOPK])
        ecol = sb("ecol", [P, 1])
        ediag = sb("ediag", [P, NCOL], f16)
        etile = sb("etile", [P, NCOL])
        etile_i = sb("etile_i", [P, NCOL], i32)
        tmp_t = sb("tmp_t", [P, NCOL])
        slot_row = sb("slot_row", [P, NCOL], i32)
        ring_row = sb("ring_row", [P, 2, UNROLL], i32)
        zero_i = sb("zero_i", [P, 1], i32)
        wjunk = sb("wjunk", [P, E])
        wslot = sb("wslot", [P, UNROLL])
        pk = [ctx.enter_context(nc.psum_tensor(f"pk{n}", [P, 512], f32)) for n in range(8)]

        l_ctx, l_x, l_gam, l_rt, l_ws = sem("l_ctx"), sem("l_x"), sem("l_gam"), sem("l_rt"), sem("l_ws")
        l_w = [sem(f"l_w{n}") for n in range(2 * E // WGRP)]
        c_pool, c_dve, c_ready = sem("c_pool"), sem("c_dve"), sem("c_ready")
        qk_mm, qk_ev = sem("qk_mm"), sem("qk_ev")
        sim_mm, sim_ev, masked = sem("sim_mm"), sem("sim_ev"), sem("masked")
        gam_rdy, st1_rdy, pre_rdy, pool_ch = sem("gam_rdy"), sem("st1_rdy"), sem("pre_rdy"), sem("pool_ch")
        chain_k = [sem(f"chain_k{i}") for i in range(2)]
        dve_ch = sem("dve_ch")
        at_mm, x1_rdy, st2_rdy, xn_rdy = sem("at_mm"), sem("x1_rdy"), sem("st2_rdy"), sem("xn_rdy")
        xnt_mm, xnt_ev, lg_mm, lg_ev = sem("xnt_mm"), sem("xnt_ev"), sem("lg_mm"), sem("lg_ev")
        sgu_mm, sgu_ev, sh_rdy, sht_mm, sht_ev = sem("sgu_mm"), sem("sgu_ev"), sem("sh_rdy"), sem("sht_mm"), sem("sht_ev")
        sy_mm, sy_ev, sacc = sem("sy_mm"), sem("sy_ev"), sem("sacc")
        d_rows = [sem(f"d_rows{i}") for i in range(2)]
        d_acc = [sem(f"d_acc{i}") for i in range(2)]
        d_zero, d_comb = sem("d_zero"), sem("d_comb")
        v_rdy, ex_rdy, comb_rdy, oh_rdy, rank_mm = sem("v_rdy"), sem("ex_rdy"), sem("comb_rdy"), sem("oh_rdy"), sem("rank_mm")
        ed_rdy, et_mm, slots_rdy, soh_rdy, toh_rdy, tab_mm = (sem(n) for n in ("ed_rdy", "et_mm", "slots_rdy", "soh_rdy", "toh_rdy", "tab_mm"))
        tab_rdy = sem("tab_rdy")
        g_done = [sem(f"g_done{u}") for u in range(UNROLL)]
        row_cp = sem("row_cp")
        t_mm, t_ev, g_mm, g_silu, h_rdy = sem("t_mm"), sem("t_ev"), sem("g_mm"), sem("g_silu"), sem("h_rdy")
        ht_mm, ht_ev, y_mm, y_ev, w_rdy = sem("ht_mm"), sem("ht_ev"), sem("y_mm"), sem("y_ev"), sem("w_rdy")
        sc_done = [sem(f"sc_done{a}") for a in range(2)]
        f_ld = [sem(f"f_ld{c}") for c in range(NB)]
        f_add, f_st = sem("f_add"), sem("f_st")

        fin = wgu_sb[:, 0:6, :].rearrange("p e w -> p (e w)")[:, 0:2 * NJ * H].rearrange("p (a j h) -> p a j h", a=2, j=NJ)

        block = ctx.enter_context(nc.Block())

        @block.sync
        def _(sp):
            sp.dma_start(ctx_sb, ctx_t).then_inc(l_ctx, 16)
            sp.dma_start(wqk_sb[:, :], wqk).then_inc(l_ctx, 16)
            sp.dma_start(x_sb[:, :, :], x.rearrange("(j p) h -> p j h", p=P)).then_inc(l_x, 16)
            sp.dma_start(wsgu_sb[:, :], ws_gu).then_inc(l_ws, 16)
            sp.dma_start(wsd_sb[:, :], ws_down).then_inc(l_ws, 16)
            for n in range(E // WGRP):
                e0 = n * WGRP
                sp.dma_start(wgu_sb[:, e0:e0 + WGRP, :], w_gu[:, e0:e0 + WGRP, :]).then_inc(l_w[2 * n], 16)
                sp.dma_start(wd_sb[:, e0:e0 + WGRP, :], w_down[:, e0:e0 + WGRP, :]).then_inc(l_w[2 * n + 1], 16)
            sp.wait_ge(c_ready, 1)
            sp.dma_start(rows_dram[TOK:ROWS, :], zero_sb[:, :]).then_inc(d_zero, 16)
            for j in range(NJ):
                sp.dma_start(acc_dram[1][j * P:(j + 1) * P, :], zero_sb[:, 0:H]).then_inc(d_zero, 16)
            for b in range(NB):
                for i in range(2):
                    r0 = (2 * b + i) * P
                    sp.wait_ge(xn_rdy, 2 * b + i + 1)
                    sp.dma_start(rows_dram[r0:r0 + P, 0:H], xn_sb[:, i, :]).then_inc(d_rows[i], 16)
                for i in range(2):
                    r0 = (2 * b + i) * P
                    sp.wait_ge(sacc, 2 * b + i + 1)
                    sp.dma_start(acc_dram[0][r0:r0 + P, :], y_sb[:, i, :]).then_inc(d_acc[i], 16)
            for a in range(2):
                sp.wait_ge(sc_done[a], 16 * (GROUPS * UNROLL // 2 + 1))
            sp.wait_ge(y_mm, GROUPS * UNROLL)
            sp.wait_ge(g_mm, GROUPS * UNROLL + 2)
            for b in range(NB):
                for a in range(2):
                    sp.dma_start(fin[:, a, 2 * b:2 * b + 2, :],
                                 acc_dram[a][b * N:(b + 1) * N, :].rearrange("(j p) h -> p j h", p=P)).then_inc(f_ld[b], 16)
            for b in range(NB):
                sp.wait_ge(f_add, b + 1)
                sp.dma_start(out[b * N:(b + 1) * N, :].rearrange("(j p) h -> p j h", p=P),
                             fin[:, 0, 2 * b:2 * b + 2, :]).then_inc(f_st, 16)
            sp.wait_ge(f_st, 16 * NB)

        @block.gpsimd
        def _(pool):
            pool.memset(zero_sb[:, :], 0.0).then_inc(c_ready, 1)
            pool.memset(half[:, :], -0.5).then_inc(c_pool, 1)
            pool.memset(ident[:, :], 0.0).then_inc(c_pool, 1)
            pool.memset(ones_h[:, :], 1.0).then_inc(c_pool, 1)
            pool.memset(ones_f[:, :], 1.0).then_inc(c_pool, 1)
            pool.memset(zero_i[:, :], 0).then_inc(c_pool, 1)
            pool.iota(iota_i, [[1, P]], base=0, channel_multiplier=0).then_inc(c_pool, 1)
            pool.iota(pidx_i[:, :], [[P, NJ]], base=0, channel_multiplier=1).then_inc(c_pool, 1)
            pool.wait_ge(c_ready, 1)
            for a in range(2):
                pool.dma_start(acc_dram[a][TOK:ROWS, :], zero_sb[:, 0:H]).then_inc(sc_done[a], 16)
            pool.wait_ge(c_pool, 7)
            pool.affine_select(out=ident[:, :], in_=ident[:, :], compare_op=ALU.not_equal, fill=1.0, base=0,
                               pattern=[[-1, P]], channel_multiplier=1).then_inc(c_pool, 1)
            pool.affine_select(out=before_h[:, :], in_=ones_h[:, :], compare_op=ALU.is_gt, fill=0.0, base=0,
                               pattern=[[1, P]], channel_multiplier=-1).then_inc(c_pool, 1)
            pool.tensor_copy(iota_f[:, :], iota_i).then_inc(c_pool, 1)
            pool.tensor_copy(iota_h[:, :], iota_i).then_inc(c_pool, 1)
            pool.tensor_copy(pidx[:, :], pidx_i[:, 0:1]).then_inc(c_pool, 1)
            pool.tensor_scalar(tok1[:, :], pidx_i[:, :], 1.0, None, ALU.add).then_inc(c_pool, 1)
            pool.tensor_scalar(pad_row[:, :], pidx_i[:, 0:1], float(TOK + 1), None, ALU.add).then_inc(c_pool, 1)
            pool.wait_ge(gam_rdy, 1)
            pool.tensor_scalar(gam[:, 2:3], gam[:, 1:2], -1.0, 1.0, ALU.mult, ALU.add).then_inc(c_pool, 1)
            pool.tensor_scalar(gam[:, 3:4], gam[:, 1:2], 0.5, None, ALU.mult).then_inc(c_pool, 1)
            pool.wait_ge(c_pool, 16)
            chain = [0]

            def link(ins):
                chain[0] += 1
                ins.then_inc(pool_ch, 1)
                pool.wait_ge(pool_ch, chain[0])

            def rstd(t, mean, var, n):
                link(pool.tensor_scalar(t[:, 0, :], var, EPS, None, ALU.add))
                link(pool.tensor_tensor(out=t[:, 1, :], in0=t[:, 0, :], in1=half[:, 0:1].to_broadcast([P, n]), op=ALU.pow))
                link(pool.tensor_tensor(out=t[:, 2, :], in0=t[:, 1, :], in1=t[:, 1, :], op=ALU.mult))
                link(pool.tensor_tensor(out=t[:, 3, :], in0=t[:, 2, :], in1=t[:, 0, :], op=ALU.mult))
                link(pool.tensor_scalar(t[:, 2, :], t[:, 3, :], -0.5, 1.5, ALU.mult, ALU.add))
                link(pool.tensor_scalar(t[:, 4, :], mean, -1.0, None, ALU.mult))
                link(pool.tensor_tensor(out=t[:, 1, :], in0=t[:, 1, :], in1=t[:, 2, :], op=ALU.mult))

            pool.wait_ge(st1_rdy, 1)
            rstd(r1, mv1[:, :, 0], mv1[:, :, 1], NJ)
            link(pool.tensor_scalar(r1[:, 5, :], r1[:, 1, :], gam[:, 2:3], None, ALU.mult))
            link(pool.tensor_tensor(out=r1[:, 3, :], in0=r1[:, 5, :], in1=r1[:, 4, :], op=ALU.mult))
            link(pool.tensor_scalar(r1[:, 2, :], r1[:, 5, :], 1.0, None, ALU.add))
            for j in range(NJ):
                pool.tensor_scalar(x_sb[:, j, :], x_sb[:, j, :], r1[:, 2, j:j + 1], r1[:, 3, j:j + 1],
                                   ALU.mult, ALU.add).then_inc(pre_rdy, 1)
            for b in range(NB):
                pool.wait_ge(st2_rdy, b + 1)
                rstd(r2, mv2[:, :, 0], mv2[:, :, 1], 2)
                for i in range(2):
                    if b:
                        pool.wait_ge(xnt_mm, 2 * b - 1 + i)
                        pool.wait_ge(d_rows[i], 16 * b)
                    pool.tensor_scalar(xn_sb[:, i, :], x_sb[:, 2 * b + i, :], r2[:, 4, i:i + 1], r2[:, 1, i:i + 1],
                                       ALU.add, ALU.mult).then_inc(xn_rdy, 1)
                for i in range(2):
                    n = 2 * b + i
                    pool.wait_ge(sgu_ev, n + 1)
                    if n >= 2:
                        pool.wait_ge(sht_mm, n - 1)
                    link(pool.tensor_tensor(out=h_sb[:, i, :], in0=gu_cp[:, 0:I], in1=sg_sb[:, 0, :], op=ALU.mult))
                    pool.tensor_tensor(out=h_sb[:, i, :], in0=h_sb[:, i, :], in1=gu_cp[:, I:GU], op=ALU.mult).then_inc(sh_rdy, 1)
                for i in range(2):
                    n = 2 * b + i
                    pool.wait_ge(sy_ev, n + 1)
                    pool.tensor_tensor(out=y_sb[:, i, :], in0=y_sb[:, i, :], in1=x_sb[:, n, :], op=ALU.add).then_inc(sacc, 1)
            pool.wait_ge(slots_rdy, 1)
            for c in range(NJ * TOPK):
                last = pool.tensor_scalar(tile_oh[:, c, :], iota_h[:, 0:NCOL], sl_p[:, 1, c:c + 1],
                                          tok1[:, c // TOPK:c // TOPK + 1], ALU.is_equal, ALU.mult)
            last.then_inc(toh_rdy, 1)

            def gather(t, u, static):
                if static:
                    link(pool.tensor_tensor(out=ring_row[:, 0, u:u + 1], in0=slot_row[:, t:t + 1], in1=zero_i[:, :], op=ALU.add))
                else:
                    pool.tensor_tensor(out=ring_row[:, 0, u:u + 1], in0=slot_row[:, bass.ds(t, 1)], in1=zero_i[:, :],
                                       op=ALU.add).then_inc(row_cp, 1)
                    pool.wait_ge(row_cp, 1)
                pool.indirect_dma_start(xg_sb[:, u, :], None, rows_dram,
                                        bass.IndirectOffsetOnAxis(ap=ring_row[:, 0, u:u + 1].bitcast(u32), axis=0)).then_inc(g_done[u], 16)
                if not static:
                    pool.sem_clear(row_cp)

            pool.wait_ge(tab_rdy, 1)
            pool.wait_ge(d_zero, 16 * (NJ + 1))
            pool.wait_ge(d_comb, 16)
            for i in range(2):
                pool.wait_ge(d_rows[i], 16 * NB)
                pool.wait_ge(d_acc[i], 16 * NB)
            for t in range(LEAD + 2):
                if t >= UNROLL:
                    pool.wait_ge(t_mm, t - UNROLL + 1)
                    pool.wait_ge(w_rdy, t - UNROLL + 1)
                gather(t, t % UNROLL, True)
            with pool.Fori(0, GROUPS) as g:
                for k in range(UNROLL):
                    t = g * UNROLL + k
                    v = (k + 5) % UNROLL
                    pool.wait_ge(t_mm, g * UNROLL + k + 2)
                    pool.wait_ge(w_rdy, g * UNROLL + k + 2)
                    gather(t + 5, v, False)
                    pool.wait_ge(y_ev, g * UNROLL + k + 2)
                    if k < 2:
                        pool.wait_ge(sc_done[k % 2], g * (8 * UNROLL) + 16)
                    else:
                        pool.wait_ge(sc_done[k % 2], g * (8 * UNROLL) + 32)
                    pool.tensor_tensor(out=ring_row[:, 1, k:k + 1], in0=slot_row[:, bass.ds(t, 1)], in1=zero_i[:, :],
                                       op=ALU.add).then_inc(row_cp, 1)
                    pool.wait_ge(row_cp, 1)
                    pool.indirect_dma_start(acc_dram[k % 2], bass.IndirectOffsetOnAxis(ap=ring_row[:, 1, k:k + 1].bitcast(u32), axis=0),
                                            y_sb[:, k % 2, :], None, compute_op=ALU.add).then_inc(sc_done[k % 2], 16)
                    pool.sem_clear(row_cp)
            last_tile = GROUPS * UNROLL + LEAD + 1
            for u in range(UNROLL):
                pool.wait_ge(g_done[u], 16 * ((last_tile - u) // UNROLL + 1))

        @block.scalar
        def _(act):
            act.dma_start(gam[:, 0:1], gamma.to_broadcast([P, 1])).then_inc(l_gam, 16)
            act.dma_start(rw_sb[:, :], router_w).then_inc(l_rt, 16)
            act.dma_start(rb_sb[:, :], router_b.to_broadcast([P, E])).then_inc(l_rt, 16)
            act.wait_ge(l_gam, 16)
            act.activation(gam[:, 1:2], gam[:, 0:1], ACT.Sigmoid).then_inc(gam_rdy, 1)

            def qk_copy(hf):
                for m, dst in enumerate((qt_sb, kt_sb)):
                    act.wait_ge(qk_mm, 2 * hf + m + 1)
                    act.activation(dst[:, hf * 512:(hf + 1) * 512], pk[4 + 2 * hf + m][0:DC, :], ACT.Copy).then_inc(qk_ev, 1)

            def sims(b):
                for i in range(2):
                    act.wait_ge(sim_mm, 2 * b + i + 1)
                    if b:
                        act.wait_ge(masked, 2 * b - 1 + i)
                    act.activation(s_sb[:, i, :], pk[1 + i][:, 0:N], ACT.Copy).then_inc(sim_ev, 1)
                    act.activation(sig_sb[:, i, :], pk[1 + i][:, 0:N], ACT.Sigmoid, scale=SIM_SCALE).then_inc(sim_ev, 1)

            qk_copy(0)
            sims(0)
            qk_copy(1)
            for b in range(NB):
                if b + 1 < NB:
                    sims(b + 1)
                for i in range(2):
                    n = 2 * b + i
                    act.wait_ge(xnt_mm, n + 1)
                    if n >= 2:
                        act.wait_ge(sgu_mm, n - 1)
                    act.activation(xt_sb[:, i, :], pk[4][:, 0:KH * P], ACT.Copy).then_inc(xnt_ev, 1)
                for i in range(2):
                    n = 2 * b + i
                    act.wait_ge(sgu_mm, n + 1)
                    if n:
                        act.wait_ge(sh_rdy, n)
                    act.activation(sg_sb[:, 0, :], pk[6][:, 0:I], ACT.Sigmoid)
                    act.activation(gu_cp[:, :], pk[6][:, 0:GU], ACT.Copy).then_inc(sgu_ev, 1)
                for i in range(2):
                    n = 2 * b + i
                    act.wait_ge(sht_mm, n + 1)
                    act.activation(ht_sb[:, i, :], pk[7][0:IC, 0:2 * P], ACT.Copy).then_inc(sht_ev, 1)
                    act.wait_ge(sy_mm, n + 1)
                    if b:
                        act.wait_ge(d_acc[i], 16 * b)
                    act.activation(y_sb[:, i, :], pk[7][:, 2 * P:2 * P + H], ACT.Copy).then_inc(sy_ev, 1)
            act.wait_ge(v_rdy, 1)
            act.activation(ex[:, :, :], ex[:, :, :], ACT.Exp).then_inc(ex_rdy, 1)
            act.wait_ge(comb_rdy, 1)
            act.dma_start(rows_dram[0:TOK, H:XW].rearrange("(j p) e -> p j e", p=P), comb[:, :, :]).then_inc(d_comb, 16)
            act.preload_act_table(ACT.Silu)

            for t in range(2):
                act.wait_ge(g_mm, t + 1)
                act.activation(sg_sb[:, t, :], pk[2 + t][:, 0:I], ACT.Silu).then_inc(g_silu, 1)
            act.wait_ge(ht_mm, 1)
            act.activation(ht_sb[:, 0, :], pk[4][0:IC, 0:2 * P], ACT.Copy).then_inc(ht_ev, 1)
            act.sem_inc(y_ev, 1)
            with act.Fori(0, GROUPS) as g:
                for k in range(UNROLL):
                    act.wait_ge(g_mm, g * UNROLL + k + 3)
                    act.wait_ge(h_rdy, g * UNROLL + k + 1)
                    act.activation(sg_sb[:, k % 2, :], pk[2 + k % 2][:, 0:I], ACT.Silu).then_inc(g_silu, 1)
                    act.wait_ge(ht_mm, g * UNROLL + k + 2)
                    act.activation(ht_sb[:, (k + 1) % 2, :], pk[4 + (k + 1) % 2][0:IC, 0:2 * P], ACT.Copy).then_inc(ht_ev, 1)
                    act.wait_ge(y_mm, g * UNROLL + k + 1)
                    act.wait_ge(w_rdy, g * UNROLL + k + 1)
                    if k < 2:
                        act.wait_ge(sc_done[k % 2], g * (8 * UNROLL) + 16)
                    else:
                        act.wait_ge(sc_done[k % 2], g * (8 * UNROLL) + 32)
                    act.activation(y_sb[:, k % 2, :], pk[6 + k % 2][:, 0:H], ACT.Copy, scale=wslot[:, k:k + 1]).then_inc(y_ev, 1)

        @block.vector
        def _(dve):
            dve.wait_ge(l_x, 16)
            for j in range(NJ):
                last = dve.bn_stats(st1[:, j, :], x_sb[:, j, :])
            last.then_inc(dve_ch, 1)
            dve.wait_ge(dve_ch, 1)
            for j in range(NJ):
                last = dve.bn_aggr(mv1[:, j, :], st1[:, j, :])
            last.then_inc(st1_rdy, 1)
            chain = [1]
            count = [0, 0]

            def link(ins):
                chain[0] += 1
                ins.then_inc(dve_ch, 1)
                dve.wait_ge(dve_ch, chain[0])

            def step(i, make):
                if count[i]:
                    dve.wait_ge(chain_k[i], count[i])
                count[i] += 1
                make().then_inc(chain_k[i], 1)

            def x1(b):
                dve.wait_ge(at_mm, b + 1)
                dve.wait_ge(pre_rdy, 2 * b + 2)
                dve.wait_ge(c_pool, 16)
                for i in range(2):
                    j = 2 * b + i
                    last = dve.scalar_tensor_tensor(out=x_sb[:, j, :], in0=pk[3][:, i * N:(i + 1) * N], scalar=gam[:, 3:4],
                                                    in1=x_sb[:, j, :], op0=ALU.mult, op1=ALU.add)
                chain[0] += 1
                last.then_inc(dve_ch, 1)
                dve.wait_ge(dve_ch, chain[0])
                if b:
                    dve.wait_ge(xn_rdy, 2 * b)
                for i in range(2):
                    last = dve.bn_stats(st2[:, i, :], x_sb[:, 2 * b + i, :])
                link(last)
                for i in range(2):
                    last = dve.bn_aggr(mv2[:, i, :], st2[:, i, :])
                last.then_inc(st2_rdy, 1)

            def router(b):
                dve.wait_ge(lg_mm, 2 * b + 2)
                dve.wait_ge(l_rt, 32)
                chain[0] += 1
                dve.tensor_tensor(out=lg_sb[:, :, :], in0=pk[5][:, 0:2 * E].rearrange("p (i e) -> p i e", i=2),
                                  in1=rb_sb[:, :].rearrange("p (o e) -> p o e", o=1).to_broadcast([P, 2, E]),
                                  op=ALU.add).then_inc(dve_ch, 1)
                dve.wait_ge(dve_ch, chain[0])
                for i in range(2):
                    last = dve.max(v8[:, 2 * b + i, :], lg_sb[:, i, :])
                chain[0] += 1
                last.then_inc(dve_ch, 1)
                dve.wait_ge(dve_ch, chain[0])
                for i in range(2):
                    last = dve.max_index(i8[:, 2 * b + i, :], v8[:, 2 * b + i, :], lg_sb[:, i, :])
                last.then_inc(lg_ev, 1)

            full = (KTH - 1) // 8
            for b in range(NB):
                for r in range(full + 1):
                    for i in range(2):
                        if r == 0:
                            dve.wait_ge(sim_ev, 4 * b + 2 * i + 1)
                            src = s_sb[:, i, :]
                        else:
                            src = work_sb[:, i, :]
                        step(i, lambda: dve.max(m8[:, i, :], src))
                    if r < full:
                        for i in range(2):
                            src = s_sb[:, i, :] if r == 0 else work_sb[:, i, :]
                            step(i, lambda: dve.match_replace(out=work_sb[:, i, :], in_to_replace=m8[:, i, :],
                                                              in_values=src, imm_value=NEG))
                    if b and r == 3:
                        x1(b - 1)
                    if b and r == 8:
                        router(b - 1)
                kth = (KTH - 1) % 8
                for i in range(2):
                    dve.wait_ge(chain_k[i], count[i])
                    dve.wait_ge(sim_ev, 4 * b + 2 * i + 2)
                    if b:
                        dve.wait_ge(at_mm, b)
                    dve.scalar_tensor_tensor(out=a_sb[:, i, :], in0=s_sb[:, i, :], scalar=m8[:, i, kth:kth + 1],
                                             in1=sig_sb[:, i, :], op0=ALU.is_ge, op1=ALU.mult).then_inc(masked, 1)
            dve.wait_ge(masked, 2 * NB)
            x1(NB - 1)
            router(NB - 1)

            dve.wait_ge(lg_ev, NB)
            dve.tensor_tensor(out=ex[:, :, :], in0=v8[:, :, 0:TOPK], in1=v8[:, :, 0:1].to_broadcast([P, NJ, TOPK]),
                              op=ALU.subtract).then_inc(v_rdy, 1)
            link(dve.tensor_copy(idx_f[:, :, :], i8[:, :, 0:TOPK]))
            iota_b = iota_f[:, 0:E].rearrange("p (o e) -> p o e", o=1).to_broadcast([P, NJ * TOPK, E])
            idx_b = idx_f[:, :, :].rearrange("p j k -> p (j k)").rearrange("p (c o) -> p c o", o=1).to_broadcast([P, NJ * TOPK, E])
            dve.tensor_tensor(out=onehot, in0=iota_b, in1=idx_b, op=ALU.is_equal).then_inc(oh_rdy, 1)
            dve.wait_ge(ex_rdy, 1)
            link(dve.reduce_sum(sm[:, 0, :], ex[:, :, :], axis=AX))
            link(dve.reciprocal(sm[:, 1, :], sm[:, 0, :]))
            link(dve.tensor_scalar(sm[:, 2, :], sm[:, 1, :], ROUTE_SCALE, None, ALU.mult))
            link(dve.tensor_tensor(out=rw[:, :, :], in0=ex[:, :, :],
                                   in1=sm[:, 2, :].rearrange("p (j o) -> p j o", o=1).to_broadcast([P, NJ, TOPK]), op=ALU.mult))
            dve.wait_ge(oh_rdy, 1)
            rw_b = rw[:, :, :].rearrange("p j k -> p (j k)").rearrange("p (c o) -> p c o", o=1).to_broadcast([P, NJ * TOPK, E])
            link(dve.tensor_tensor(out=prod, in0=onehot, in1=rw_b, op=ALU.mult))
            dve.tensor_reduce(comb[:, :, :], prod.rearrange("p (j k) e -> p j e k", k=TOPK), axis=AX, op=ALU.add).then_inc(comb_rdy, 1)
            dve.wait_ge(rank_mm, 1)
            link(dve.tensor_scalar(cnt_i[:, 0, :], pk[0][:, NJ * E:NJ * E + E], float(P - 1), None, ALU.add))
            link(dve.tensor_scalar(cnt_i[:, 1, :], cnt_i[:, 0, :], 7, None, ALU.logical_shift_right))
            link(dve.tensor_copy(ntl[:, 0, :], cnt_i[:, 1, :]))
            link(dve.tensor_tensor_scan(ntl[:, 1, :], ones_f[:, :], ntl[:, 0, :], 0.0, ALU.mult, ALU.add))
            link(dve.tensor_tensor(out=ntl[:, 2, :], in0=ntl[:, 1, :], in1=ntl[:, 0, :], op=ALU.subtract))
            link(dve.tensor_scalar(ntl[:, 3, :], ntl[:, 2, :], float(P), None, ALU.mult))
            first_b = ntl[:, 3, :].rearrange("p (o e) -> p o e", o=1).to_broadcast([P, NJ, E])
            link(dve.tensor_tensor(out=srank[:, :, :], in0=pk[0][:, 0:NJ * E].rearrange("p (j e) -> p j e", j=NJ), in1=first_b, op=ALU.add))
            srank_b = srank[:, :, :].rearrange("p j (o e) -> p j o e", o=1).to_broadcast([P, NJ, TOPK, E])
            dve.wait_ge(comb_rdy, 1)
            link(dve.tensor_tensor(out=prod.rearrange("p (j k) e -> p j k e", k=TOPK),
                                   in0=onehot.rearrange("p (j k) e -> p j k e", k=TOPK), in1=srank_b, op=ALU.mult))
            link(dve.reduce_sum(sl_f[:, :], prod, axis=AX))
            link(dve.tensor_copy(sl_i[:, 0, :], sl_f[:, :]))
            dve.tensor_scalar(sl_i[:, 1, :], sl_i[:, 0, :], P - 1, None, ALU.bitwise_and)
            link(dve.tensor_scalar(sl_i[:, 2, :], sl_i[:, 0, :], 7, None, ALU.logical_shift_right))
            dve.tensor_copy(sl_p[:, :, :], sl_i[:, 1:3, :]).then_inc(slots_rdy, 1)
            link(dve.tensor_scalar(wjunk[:, :], ntl[:, 1, :], pidx[:, 0:1], 0.0, ALU.is_le, ALU.add, accum_out=ecol[:, :]))
            dve.tensor_scalar(ediag[:, :], ident[:, 0:NCOL], ecol[:, 0:1], None, ALU.mult).then_inc(ed_rdy, 1)
            dve.wait_ge(slots_rdy, 1)
            for c in range(NJ * TOPK):
                last = dve.tensor_scalar(slot_oh[:, c, :], iota_h[:, :], sl_p[:, 0, c:c + 1], None, ALU.is_equal)
            last.then_inc(soh_rdy, 1)
            dve.wait_ge(et_mm, 1)
            dve.tensor_copy(etile[:, :], pk[2][:, 0:NCOL])
            dve.tensor_scalar(etile_i[:, :], pk[2][:, 0:NCOL], float(E - 1), None, ALU.min)
            dve.wait_ge(tab_mm, 1)
            link(dve.tensor_scalar(tmp_t[:, :], pk[1][:, 0:NCOL], 0.0, pad_row[:, 0:1], ALU.is_equal, ALU.mult))
            dve.scalar_tensor_tensor(out=slot_row[:, :], in0=pk[1][:, 0:NCOL], scalar=-1.0, in1=tmp_t[:, :],
                                     op0=ALU.add, op1=ALU.add).then_inc(tab_rdy, 1)

            def weights_of(expert_col, u):
                dve.scalar_tensor_tensor(out=wjunk[:, :], in0=iota_f[:, 0:E], scalar=expert_col,
                                         in1=xg_sb[:, u, H:XW], op0=ALU.is_equal, op1=ALU.mult,
                                         accum_out=wslot[:, u:u + 1]).then_inc(w_rdy, 1)

            def rows_out(k):
                dve.tensor_copy(xt_sb[:, k % 2, :], pk[k % 2][:, 0:KH * P]).then_inc(t_ev, 1)

            def gated(k):
                dve.tensor_tensor(out=h_sb[:, k % 2, :], in0=pk[2 + k % 2][:, I:GU], in1=sg_sb[:, k % 2, :],
                                  op=ALU.mult).then_inc(h_rdy, 1)

            dve.wait_ge(tab_rdy, 1)
            for t in range(3):
                if t:
                    dve.wait_ge(g_silu, t)
                    gated(t - 1)
                dve.wait_ge(g_done[t], 16)
                weights_of(etile[:, t:t + 1], t)
                dve.wait_ge(t_mm, t + 1)
                if t == 2:
                    dve.wait_ge(g_mm, 1)
                rows_out(t)
            with dve.Fori(0, GROUPS) as g:
                for k in range(UNROLL):
                    u = (k + 3) % UNROLL
                    dve.wait_ge(g_silu, g * UNROLL + k + 3)
                    dve.wait_ge(ht_mm, g * UNROLL + k + 1)
                    gated(k)
                    dve.wait_ge(g_done[u], g * 16 + 16 * ((k + 3) // UNROLL + 1))
                    dve.wait_ge(y_ev, g * UNROLL + k + 1)
                    weights_of(etile[:, bass.ds(g * UNROLL + k + 3, 1)], u)
                    dve.wait_ge(t_mm, g * UNROLL + k + 4)
                    dve.wait_ge(g_mm, g * UNROLL + k + 2)
                    rows_out(k + 1)
            for b in range(NB):
                dve.wait_ge(f_ld[b], 32)
                dve.tensor_tensor(out=fin[:, 0, 2 * b:2 * b + 2, :], in0=fin[:, 0, 2 * b:2 * b + 2, :],
                                  in1=fin[:, 1, 2 * b:2 * b + 2, :], op=ALU.add).then_inc(f_add, 1)

        @block.tensor
        def _(pe):
            pe.wait_ge(l_ctx, 32)

            def qk(hf):
                for m in range(2):
                    pe.matmul(pk[4 + 2 * hf + m][0:DC, :], wqk_sb[:, m * DC:(m + 1) * DC], ctx_sb[:, hf * 512:(hf + 1) * 512],
                              start=True, stop=True).then_inc(qk_mm, 1)

            def sims(b):
                pe.wait_ge(qk_ev, 2 * (b // 2) + 2)
                for i in range(2):
                    if b:
                        pe.wait_ge(sim_ev, 4 * (b - 1) + 2 * i + 2)
                    r0 = (2 * b + i) * P
                    pe.matmul(pk[1 + i][:, 0:N], qt_sb[:, r0:r0 + P], kt_sb[:, b * N:(b + 1) * N],
                              start=True, stop=True).then_inc(sim_mm, 1)

            qk(0)
            sims(0)
            qk(1)
            pe.wait_ge(c_pool, 16)
            pe.wait_ge(qk_ev, 4)
            for b in range(NB):
                if b + 1 < NB:
                    sims(b + 1)
                pe.wait_ge(masked, 2 * b + 2)
                if b:
                    pe.wait_ge(st2_rdy, b)
                for i in range(2):
                    o = pk[3][:, i * N:(i + 1) * N]
                    pe.matmul(o, ident[:, :], a_sb[:, i, :], start=True, stop=False)
                    for c in range(2):
                        last = pe.matmul(pk[3][:, i * N + c * P:i * N + (c + 1) * P], a_sb[:, c, i * P:(i + 1) * P], ident[:, :],
                                         start=False, stop=c == 1)
                last.then_inc(at_mm, 1)
                for i in range(2):
                    n = 2 * b + i
                    pe.wait_ge(xn_rdy, n + 1)
                    if n:
                        pe.wait_ge(xnt_ev, n)
                    for c in range(KH):
                        last = pe.transpose(pk[4][:, c * P:(c + 1) * P], xn_sb[:, i, c * P:(c + 1) * P], ident[:, :])
                    last.then_inc(xnt_mm, 1)
                if b:
                    pe.wait_ge(lg_ev, b)
                pe.wait_ge(l_rt, 32)
                for i in range(2):
                    pe.wait_ge(xnt_ev, 2 * b + i + 1)
                    for c in range(KH):
                        last = pe.matmul(pk[5][:, i * E:(i + 1) * E], xt_sb[:, i, c * P:(c + 1) * P], rw_sb[:, c * E:(c + 1) * E],
                                         start=c == 0, stop=c == KH - 1)
                    last.then_inc(lg_mm, 1)
                pe.wait_ge(l_ws, 32)
                for i in range(2):
                    n = 2 * b + i
                    if n:
                        pe.wait_ge(sgu_ev, n)
                    for c in range(KH):
                        last = pe.matmul(pk[6][:, 0:GU], xt_sb[:, i, c * P:(c + 1) * P], wsgu_sb[:, c * GU:(c + 1) * GU],
                                         start=c == 0, stop=c == KH - 1)
                    last.then_inc(sgu_mm, 1)
                for i in range(2):
                    n = 2 * b + i
                    pe.wait_ge(sh_rdy, n + 1)
                    if n:
                        pe.wait_ge(sy_ev, n)
                    for c in range(2):
                        last = pe.transpose(pk[7][0:IC, c * P:(c + 1) * P], h_sb[:, i, c * IC:(c + 1) * IC], ident[:, :])
                    last.then_inc(sht_mm, 1)
                    pe.wait_ge(sht_ev, n + 1)
                    for c in range(2):
                        last = pe.matmul(pk[7][:, 2 * P:2 * P + H], ht_sb[:, i, c * P:(c + 1) * P], wsd_sb[:, c * H:(c + 1) * H],
                                         start=c == 0, stop=c == 1)
                    last.then_inc(sy_mm, 1)
            pe.wait_ge(oh_rdy, 1)
            oh = onehot.rearrange("p (j k) e -> p j k e", k=TOPK)
            for k in range(TOPK):
                pe.matmul(pk[0][:, 0:NJ * E], before_h[:, :], oh[:, :, k, :], start=k == 0, stop=False, skip_group_check=True)
            for j in range(NJ):
                for k in range(TOPK):
                    last = pe.matmul(pk[0][:, (j + 1) * E:(NJ + 1) * E].rearrange("p (m e) -> p m e", e=E), ones_h[:, :],
                                     oh[:, j:j + 1, k, :].to_broadcast([P, NJ - j, E]), start=False,
                                     stop=(j == NJ - 1 and k == TOPK - 1), skip_group_check=True)
            last.then_inc(rank_mm, 1)
            pe.wait_ge(ed_rdy, 1)
            pe.matmul(pk[2][:, 0:NCOL], ones_h[:, :], ediag[:, :], start=True, stop=True).then_inc(et_mm, 1)
            pe.wait_ge(soh_rdy, 1)
            pe.wait_ge(toh_rdy, 1)
            for c in range(NJ * TOPK):
                last = pe.matmul(pk[1][:, 0:NCOL], slot_oh[:, c, :], tile_oh[:, c, :], start=c == 0, stop=c == NJ * TOPK - 1)
            last.then_inc(tab_mm, 1)
            for s in l_w:
                pe.wait_ge(s, 16)

            def rows_t(k, u):
                for c in range(KH):
                    last = pe.transpose(pk[k % 2][:, c * P:(c + 1) * P], xg_sb[:, u, c * P:(c + 1) * P], ident[:, :])
                last.then_inc(t_mm, 1)

            def gate_up(k, e):
                for c in range(KH):
                    last = pe.matmul(pk[2 + k % 2][:, 0:GU], xt_sb[:, k % 2, c * P:(c + 1) * P],
                                     wgu_sb[:, bass.ds(e, 1), c * GU:(c + 1) * GU], start=c == 0, stop=c == KH - 1)
                last.then_inc(g_mm, 1)

            def h_t(k):
                for c in range(2):
                    last = pe.transpose(pk[4 + k % 2][0:IC, c * P:(c + 1) * P], h_sb[:, k % 2, c * IC:(c + 1) * IC], ident[:, :])
                last.then_inc(ht_mm, 1)

            def down(k, e):
                for c in range(2):
                    last = pe.matmul(pk[6 + k % 2][:, 0:H], ht_sb[:, k % 2, c * P:(c + 1) * P],
                                     wd_sb[:, bass.ds(e, 1), c * H:(c + 1) * H], start=c == 0, stop=c == 1)
                last.then_inc(y_mm, 1)

            def expert(t):
                return pe.value_load(etile_i[0:1, t:t + 1] if isinstance(t, int) else etile_i[0:1, bass.ds(t, 1)], min_val=0, max_val=E - 1)

            pe.wait_ge(tab_rdy, 1)
            for t in range(2):
                pe.wait_ge(g_done[t], 16)
                rows_t(t, t)
            e_up = expert(0)
            pe.wait_ge(t_ev, 1)
            gate_up(0, e_up)
            pe.wait_ge(g_done[2], 16)
            rows_t(0, 2)
            e_up = expert(1)
            pe.wait_ge(t_ev, 2)
            gate_up(1, e_up)
            pe.wait_ge(h_rdy, 1)
            h_t(0)
            with pe.Fori(0, GROUPS) as g:
                for k in range(UNROLL):
                    u = (k + 3) % UNROLL
                    e_up, e_down = expert(g * UNROLL + k + 2), expert(g * UNROLL + k)
                    pe.wait_ge(t_ev, g * UNROLL + k + 3)
                    pe.wait_ge(h_rdy, g * UNROLL + k + 1)
                    gate_up(k, e_up)
                    pe.wait_ge(h_rdy, g * UNROLL + k + 2)
                    pe.wait_ge(ht_ev, g * UNROLL + max(k, 1))
                    h_t(k + 1)
                    pe.wait_ge(ht_ev, g * UNROLL + k + 1)
                    pe.wait_ge(y_ev, g * UNROLL + max(k, 1))
                    down(k, e_down)
                    pe.wait_ge(g_done[u], g * 16 + 16 * ((k + 3) // UNROLL + 1))
                    rows_t(k + 1, u)


def kernel(x, ctx_512, L0_xattn_Wq, L0_xattn_Wk, L0_xattn_gamma_raw, L0_ffn_router_w, L0_ffn_router_b,
           L0_ffn_gate_w, L0_ffn_up_w, L0_ffn_down_w, L0_ffn_shared_gate_w, L0_ffn_shared_up_w, L0_ffn_shared_down_w):
    import numpy as np
    import concourse.bacc as bacc
    from concourse import mybir as mb
    from concourse.bass_utils import run_bass_kernel_spmd

    def chunks(w, k):
        return np.ascontiguousarray(w.T.reshape(-1, k, w.shape[0]).transpose(1, 0, 2).reshape(k, -1))

    gu = np.concatenate([np.asarray(L0_ffn_gate_w), np.asarray(L0_ffn_up_w)], axis=1)
    gu = gu.transpose(2, 0, 1).reshape(KH, P, E, GU).transpose(1, 2, 0, 3).reshape(P, E, KH * GU)
    dn = np.asarray(L0_ffn_down_w).transpose(2, 0, 1).reshape(2, IC, E, H).transpose(1, 2, 0, 3).reshape(IC, E, 2 * H)
    arrays = {
        "x_dram": np.asarray(x).reshape(TOK, H),
        "ctx_t_dram": np.asarray(ctx_512).reshape(TOK, DC).T,
        "wqk_dram": np.concatenate([np.asarray(L0_xattn_Wq).T, np.asarray(L0_xattn_Wk).T], axis=1),
        "gamma_dram": np.asarray(L0_xattn_gamma_raw).reshape(1, 1),
        "router_w_dram": chunks(np.asarray(L0_ffn_router_w), P),
        "router_b_dram": np.asarray(L0_ffn_router_b).reshape(1, E),
        "w_gu_dram": gu,
        "w_down_dram": dn,
        "ws_gu_dram": chunks(np.concatenate([np.asarray(L0_ffn_shared_gate_w), np.asarray(L0_ffn_shared_up_w)], axis=0), P),
        "ws_down_dram": chunks(np.asarray(L0_ffn_shared_down_w), IC),
    }
    arrays = {n: np.ascontiguousarray(a) for n, a in arrays.items()}
    nc = bacc.Bacc("TRN2", target_bir_lowering=False, num_devices=1, dynamic_dma_scratch_size=8192)
    args = [nc.dram_tensor(n, a.shape, mb.dt.from_np(a.dtype), kind="ExternalInput").ap() for n, a in arrays.items()]
    out = nc.dram_tensor("out_dram", (TOK, H), mb.dt.float32, kind="ExternalOutput").ap()
    build(nc, *args, out)
    r = run_bass_kernel_spmd(nc, [arrays], core_ids=[0])
    return r.results[0]["out_dram"].reshape(NB, N, H)
```

```python
import concourse.bass as bass
from concourse import mybir
from contextlib import ExitStack

P = 128
NB, N, H, DC = 4, 256, 256, 64
TOK = NB * N
NJ = TOK // P
E, I, TOPK = 32, 192, 4
KTH = int(N * 0.3)
EPS = 1e-5
ROUTE_SCALE = 1.8
SIM_SCALE = 1.0 / 16.0
KH = H // P
IC = I // 2
GU = 2 * I
XW = H + E
MAX_TILES = E + (TOK * TOPK - E) // P
UNROLL = 4
LEAD = 3
GROUPS = -(-MAX_TILES // UNROLL)
EARLY = (NB - 1) * 2
NCOL = 72
assert NCOL >= GROUPS * UNROLL + 2 + LEAD and NCOL % 4 == 0
ROWS = TOK + P
NEG = -3.0e38
WGRP = 4


def build(nc, x, ctx_wqk, gamma, router_w, router_b, w_gu, w_down, ws_gu, ws_down, out):
    f32, f16 = mybir.dt.float32, mybir.dt.float16
    i32, u32 = mybir.dt.int32, mybir.dt.uint32
    ALU = mybir.AluOpType
    ACT = mybir.ActivationFunctionType
    AX = mybir.AxisListType.X

    rows_dram = nc.dram_tensor("token_rows", (ROWS, XW), f32, kind="Internal").ap()
    acc_dram = [nc.dram_tensor(f"acc{a}", (ROWS, H), f32, kind="Internal").ap() for a in range(2)]

    ctx = ExitStack()
    with ctx:
        def sb(name, shape, dt=f32):
            return ctx.enter_context(nc.sbuf_tensor(name, shape, dt))

        def sem(name):
            return ctx.enter_context(nc.semaphore(name))

        wgu_sb = sb("wgu_sb", [P, E, KH * GU])
        wd_sb = sb("wd_sb", [IC, E, 2 * H])
        wsgu_sb = sb("wsgu_sb", [P, KH * GU])
        wsd_sb = sb("wsd_sb", [IC, 2 * H])
        rw_sb = sb("rw_sb", [P, KH * E])
        rb_sb = sb("rb_sb", [P, E])
        x_sb = sb("x_sb", [P, NJ, H])
        xg_sb = x_sb[:, 0:5, :].rearrange("p j h -> p (j h)")[:, 0:4 * XW].rearrange("p (u w) -> p u w", u=4)
        arena = sb("arena", [P, 4736])
        cw_sb = arena[0:DC, 0:TOK + 2 * DC]
        ctx_sb, wqk_sb = cw_sb[:, 0:TOK], cw_sb[:, TOK:]
        qt_sb = arena[0:DC, 1152:2176]
        kt_sb = arena[0:DC, 2176:3200]
        s_sb = [wgu_sb[:, E - 1, 0:2 * N].rearrange("p (i n) -> p i n", i=2), arena[:, 3200:3712].rearrange("p (i n) -> p i n", i=2)]
        sig_sb = arena[:, 3712:4224].rearrange("p (i n) -> p i n", i=2)
        a_sb = arena[:, 4224:4736].rearrange("p (i n) -> p i n", i=2)
        onehot = arena[:, 0:512].bitcast(f16).rearrange("p (c e) -> p c e", e=E)
        prod = arena[:, 512:1536].rearrange("p (c e) -> p c e", e=E)
        prod_h = arena[:, 512:1024].bitcast(f16).rearrange("p (c e) -> p c e", e=E)
        slot_oh = arena[:, 1536:3584].bitcast(f16).rearrange("p (c s) -> p c s", s=P)
        tile_oh = arena[:, 3584:3584 + 16 * NCOL].bitcast(f16).rearrange("p (c t) -> p c t", t=NCOL)
        work_sb = sb("work_sb", [P, 2, N])
        xn_sb = sb("xn_sb", [P, 2, H])
        xt_sb = sb("xt_sb", [P, 2, KH * P])
        sg_sb = sb("sg_sb", [P, 2, I])
        h_sb = sb("h_sb", [P, 2, I])
        iota_i = h_sb[:, 0, 0:P].bitcast(i32)
        ht_sb = sb("ht_sb", [IC, 2, 2 * P])
        y_sb = sb("y_sb", [P, 2, H])
        xn_of = [xn_sb, y_sb]
        gu_cp = sb("gu_cp", [P, 2, GU])
        zero_sb = gu_cp[:, 1, 0:XW]
        ident = sb("ident", [P, P])
        ones_f = sb("ones_f", [P, E])
        ones_h = sb("ones_h", [P, P], f16)
        before_h = sb("before_h", [P, P], f16)
        iota_f = sb("iota_f", [P, P])
        iota_h = sb("iota_h", [P, P], f16)
        pidx_i = sb("pidx_i", [P, NJ], i32)
        tok1 = sb("tok1", [P, NJ])
        pad_row = sb("pad_row", [P, 1])
        pidx = sb("pidx", [P, 1])
        gam = sb("gam", [P, 4])
        st1 = sb("st1", [P, NJ, 6])
        mv1 = sb("mv1", [P, NJ, 2])
        r1 = sb("r1", [P, 6, NJ])
        half = sb("half", [P, 1])
        st2 = sb("st2", [P, 2, 6])
        mv2 = sb("mv2", [P, 2, 2])
        r2 = sb("r2", [P, 5, 2])
        m8 = sb("m8", [P, 2, 8])
        lg_sb = sb("lg_sb", [P, 2, E])
        v8 = sb("v8", [P, NJ, 8])
        i8 = sb("i8", [P, NJ, 8], u32)
        idx_f = sb("idx_f", [P, NJ, TOPK])
        ex = sb("ex", [P, NJ, TOPK])
        sm = sb("sm", [P, 3, NJ])
        rw = sb("rw", [P, NJ, TOPK])
        comb = sb("comb", [P, NJ, E])
        cnt_i = sb("cnt_i", [P, 2, E], i32)
        ntl = work_sb[:, 0, 0:4 * E].rearrange("p (n e) -> p n e", e=E)
        first_h = ntl[:, 2, 0:E // 2].bitcast(f16)
        srank = work_sb[:, 1, :].rearrange("p (j e) -> p j e", e=E)
        sl_f = sb("sl_f", [P, NJ * TOPK])
        sl_i = work_sb[:, 0, 4 * E:4 * E + 3 * NJ * TOPK].bitcast(i32).rearrange("p (n c) -> p n c", n=3)
        sl_p = sb("sl_p", [P, 2, NJ * TOPK])
        ecol = sb("ecol", [P, 1])
        ediag = sb("ediag", [P, NCOL], f16)
        etile = sb("etile", [P, NCOL])
        etile_i = sb("etile_i", [P, NCOL], i32)
        tmp_t = sb("tmp_t", [P, NCOL])
        slot_row = sb("slot_row", [P, NCOL], i32)
        ring_row = sb("ring_row", [P, 2, 7], i32)
        groups_i = sb("groups_i", [P, 2], i32)
        zero_i = sb("zero_i", [P, 1], i32)
        wslot = sb("wslot", [P, UNROLL])
        pk = [ctx.enter_context(nc.psum_tensor(f"pk{n}", [P, 512], f32)) for n in range(8)]

        xnt_ps = [pk[4], pk[0]]

        l_ctx, l_gam, l_rt, l_ws = sem("l_ctx"), sem("l_gam"), sem("l_rt"), sem("l_ws")
        l_x = [sem(f"l_x{hf}") for hf in range(2)]
        l_w = [sem(f"l_w{n}") for n in range(2 * E // WGRP)]
        c_pool, c_dve, c_ready = sem("c_pool"), sem("c_dve"), sem("c_ready")
        qk_mm, qk_ev = sem("qk_mm"), sem("qk_ev")
        sim_mm, sim_ev, sig_ev, sig_rdy, masked = sem("sim_mm"), sem("sim_ev"), sem("sig_ev"), sem("sig_rdy"), sem("masked")
        gam_rdy, st1_rdy, pre_rdy, pool_ch = sem("gam_rdy"), sem("st1_rdy"), sem("pre_rdy"), sem("pool_ch")
        chain_k = [sem(f"chain_k{i}") for i in range(2)]
        dve_ch = sem("dve_ch")
        at_mm, x1_rdy, st2_rdy, xn_rdy = sem("at_mm"), sem("x1_rdy"), sem("st2_rdy"), sem("xn_rdy")
        xnt_mm, xnt_ev, lg_mm, lg_ev = sem("xnt_mm"), sem("xnt_ev"), sem("lg_mm"), sem("lg_ev")
        sgu_mm, sgu_ev, sh_rdy, sht_mm, sht_ev = sem("sgu_mm"), sem("sgu_ev"), sem("sh_rdy"), sem("sht_mm"), sem("sht_ev")
        sy_mm, sy_ev, sacc, xa_rdy = sem("sy_mm"), sem("sy_ev"), sem("sacc"), sem("xa_rdy")
        d_rows = [[sem(f"d_rows{b}{i}") for i in range(2)] for b in range(2)]
        d_acc = [sem("d_acc"), sem("d_acc_last")]
        d_zero, d_comb = sem("d_zero"), sem("d_comb")
        v_rdy, ex_rdy, comb_rdy, oh_rdy, rank_mm = sem("v_rdy"), sem("ex_rdy"), sem("comb_rdy"), sem("oh_rdy"), sem("rank_mm")
        ed_rdy, et_mm, slots_rdy, rw_rdy, toh_rdy, tab_mm = (sem(n) for n in ("ed_rdy", "et_mm", "slots_rdy", "rw_rdy", "toh_rdy", "tab_mm"))
        tab_rdy, soh_rdy, tok_rdy = sem("tab_rdy"), sem("soh_rdy"), sem("tok_rdy")
        g_done = [sem(f"g_done{u}") for u in range(UNROLL)]
        row_cp = sem("row_cp")
        t_mm, t_ev, g_mm, g_silu, h_rdy = sem("t_mm"), sem("t_ev"), sem("g_mm"), sem("g_silu"), sem("h_rdy")
        ht_mm, ht_ev, y_mm, y_ev, w_rdy = sem("ht_mm"), sem("ht_ev"), sem("y_mm"), sem("y_ev"), sem("w_rdy")
        sc_done = [sem(f"sc_done{a}") for a in range(2)]
        issued = sem("issued")
        experts_end = sem("experts_end")
        f_ld = [sem(f"f_ld{c}") for c in range(NB)]
        f_add, f_st = sem("f_add"), sem("f_st")

        fin = wgu_sb[:, 0:6, :].rearrange("p e w -> p (e w)")[:, 0:2 * NJ * H].rearrange("p (a j h) -> p a j h", a=2, j=NJ)

        block = ctx.enter_context(nc.Block())

        @block.sync
        def _(sp):
            sp.dma_start(cw_sb, ctx_wqk).then_inc(l_ctx, 16)
            for hf in range(2):
                j0 = hf * NJ // 2
                sp.dma_start(x_sb[:, j0:j0 + NJ // 2, :], x[j0 * P:(j0 + NJ // 2) * P, :].rearrange("(j p) h -> p j h", p=P)).then_inc(l_x[hf], 16)
            sp.dma_start(gam[:, 0:1], gamma.to_broadcast([P, 1])).then_inc(l_gam, 16)
            sp.dma_start(rw_sb[:, :], router_w).then_inc(l_rt, 16)
            sp.dma_start(rb_sb[:, :], router_b.to_broadcast([P, E])).then_inc(l_rt, 16)
            sp.wait_ge(c_ready, 1)
            sp.dma_start(rows_dram[TOK:ROWS, :], zero_sb).then_inc(d_zero, 16)
            for j in range(NJ):
                sp.dma_start(acc_dram[1][j * P:(j + 1) * P, :], gu_cp[:, 1, 0:H]).then_inc(d_zero, 16)
            sp.dma_start(wsgu_sb[:, :], ws_gu).then_inc(l_ws, 16)
            sp.dma_start(wsd_sb[:, :], ws_down).then_inc(l_ws, 16)

            def weights(n0, n1):
                for n in range(n0, n1):
                    e0 = n * WGRP
                    if n == E // WGRP - 1:
                        sp.wait_ge(masked, 2 * NB - 2)
                    sp.dma_start(wgu_sb[:, e0:e0 + WGRP, :], w_gu[:, e0:e0 + WGRP, :]).then_inc(l_w[2 * n], 16)
                    sp.dma_start(wd_sb[:, e0:e0 + WGRP, :], w_down[:, e0:e0 + WGRP, :]).then_inc(l_w[2 * n + 1], 16)

            def store_residual(b):
                for i in range(2):
                    n = 2 * b + i
                    sp.wait_ge(sacc, n + 1)
                    sp.dma_start(acc_dram[0][n * P:(n + 1) * P, :], x_sb[:, n, :]).then_inc(d_acc[b // (NB - 1)], 16)

            weight_groups = (2, 5, 7, 8, 8)
            weights(0, weight_groups[0])
            for b in range(NB):
                for i in range(2):
                    n = 2 * b + i
                    sp.wait_ge(xn_rdy, n + 1)
                    sp.dma_start(rows_dram[n * P:(n + 1) * P, 0:H], xn_of[b % 2][:, i, :]).then_inc(d_rows[b % 2][i], 16)
                weights(weight_groups[b], weight_groups[b + 1])
                if b:
                    store_residual(b - 1)
            sp.wait_ge(comb_rdy, 1)
            sp.dma_start(rows_dram[0:TOK, H:XW].rearrange("(j p) e -> p j e", p=P), comb[:, :, :]).then_inc(d_comb, 16)
            store_residual(NB - 1)
            sp.wait_ge(tab_rdy, 1)
            groups = sp.value_load(groups_i[0:1, 1:2], min_val=1, max_val=GROUPS)
            sp.wait_ge(experts_end, 1)
            for a in range(2):
                sp.wait_ge(sc_done[a], groups * (8 * UNROLL) + 16)
                for b in range(NB):
                    sp.dma_start(fin[:, a, 2 * b:2 * b + 2, :],
                                 acc_dram[a][b * N:(b + 1) * N, :].rearrange("(j p) h -> p j h", p=P)).then_inc(f_ld[b], 16)
            for b in range(NB):
                sp.wait_ge(f_add, b + 1)
                sp.dma_start(out[b * N:(b + 1) * N, :].rearrange("(j p) h -> p j h", p=P),
                             fin[:, 0, 2 * b:2 * b + 2, :]).then_inc(f_st, 16)
            sp.wait_ge(f_st, 16 * NB)

        @block.gpsimd
        def _(pool):
            pool.memset(zero_sb, 0.0).then_inc(c_ready, 1)
            pool.memset(half[:, :], -0.5).then_inc(c_pool, 1)
            pool.memset(ident[:, :], 0.0).then_inc(c_pool, 1)
            pool.memset(ones_h[:, :], 1.0).then_inc(c_pool, 1)
            pool.memset(ones_f[:, :], 1.0).then_inc(c_pool, 1)
            pool.memset(zero_i[:, :], 0).then_inc(c_pool, 1)
            pool.iota(iota_i, [[1, P]], base=0, channel_multiplier=0).then_inc(c_pool, 1)
            pool.iota(pidx_i[:, :], [[P, NJ]], base=0, channel_multiplier=1).then_inc(c_pool, 1)
            pool.wait_ge(c_ready, 1)
            for a in range(2):
                pool.dma_start(acc_dram[a][TOK:ROWS, :], gu_cp[:, 1, 0:H]).then_inc(sc_done[a], 16)
            pool.wait_ge(c_pool, 7)
            pool.affine_select(out=ident[:, :], in_=ident[:, :], compare_op=ALU.not_equal, fill=1.0, base=0,
                               pattern=[[-1, P]], channel_multiplier=1).then_inc(c_pool, 1)
            pool.affine_select(out=before_h[:, :], in_=ones_h[:, :], compare_op=ALU.is_gt, fill=0.0, base=0,
                               pattern=[[1, P]], channel_multiplier=-1).then_inc(c_pool, 1)
            pool.tensor_copy(iota_f[:, :], iota_i).then_inc(c_pool, 1)
            pool.tensor_copy(iota_h[:, :], iota_i).then_inc(c_pool, 1)
            pool.tensor_copy(pidx[:, :], pidx_i[:, 0:1]).then_inc(c_pool, 1)
            pool.tensor_scalar(tok1[:, :], pidx_i[:, :], 1.0, None, ALU.add).then_inc(c_pool, 1)
            pool.tensor_scalar(pad_row[:, :], pidx_i[:, 0:1], float(TOK + 1), None, ALU.add).then_inc(c_pool, 1)
            pool.wait_ge(gam_rdy, 1)
            pool.tensor_scalar(gam[:, 2:3], gam[:, 1:2], -1.0, 1.0, ALU.mult, ALU.add).then_inc(c_pool, 1)
            pool.tensor_scalar(gam[:, 3:4], gam[:, 1:2], 0.5, None, ALU.mult).then_inc(c_pool, 1)
            pool.wait_ge(c_pool, 16)
            chain = [0]

            def link(ins):
                chain[0] += 1
                ins.then_inc(pool_ch, 1)
                pool.wait_ge(pool_ch, chain[0])

            def rstd(t, mean, var, n):
                link(pool.tensor_scalar(t[:, 0, :], var, EPS, None, ALU.add))
                pool.tensor_scalar(t[:, 4, :], mean, -1.0, None, ALU.mult)
                link(pool.tensor_tensor(out=t[:, 1, :], in0=t[:, 0, :], in1=half[:, 0:1].to_broadcast([P, n]), op=ALU.pow))
                link(pool.tensor_tensor(out=t[:, 2, :], in0=t[:, 1, :], in1=t[:, 1, :], op=ALU.mult))
                link(pool.tensor_tensor(out=t[:, 3, :], in0=t[:, 2, :], in1=t[:, 0, :], op=ALU.mult))
                link(pool.tensor_scalar(t[:, 2, :], t[:, 3, :], -0.5, 1.5, ALU.mult, ALU.add))
                link(pool.tensor_tensor(out=t[:, 1, :], in0=t[:, 1, :], in1=t[:, 2, :], op=ALU.mult))

            def scale_sigmoid(b):
                for i in range(2):
                    pool.wait_ge(sig_ev, 2 * b + i + 1)
                    pool.tensor_scalar(sig_sb[:, i, :], sig_sb[:, i, :], gam[:, 3:4], None, ALU.mult).then_inc(sig_rdy, 1)

            scale_sigmoid(0)
            pool.wait_ge(st1_rdy, 1)
            rstd(r1, mv1[:, :, 0], mv1[:, :, 1], NJ)
            link(pool.tensor_scalar(r1[:, 5, :], r1[:, 1, :], gam[:, 2:3], None, ALU.mult))
            link(pool.tensor_tensor(out=r1[:, 3, :], in0=r1[:, 5, :], in1=r1[:, 4, :], op=ALU.mult))
            link(pool.tensor_scalar(r1[:, 2, :], r1[:, 5, :], 1.0, None, ALU.add))
            for j in range(NJ):
                pool.tensor_scalar(x_sb[:, j, :], x_sb[:, j, :], r1[:, 2, j:j + 1], r1[:, 3, j:j + 1],
                                   ALU.mult, ALU.add).then_inc(pre_rdy, 1)
            def add_shared(b):
                for i in range(2):
                    n = 2 * b + i
                    pool.wait_ge(sy_ev, n + 1)
                    pool.tensor_tensor(out=x_sb[:, n, :], in0=x_sb[:, n, :], in1=gu_cp[:, i, 0:H], op=ALU.add).then_inc(sacc, 1)

            def add_attention(b):
                for i in range(2):
                    pool.wait_ge(masked, 2 * b + i + 1)
                    pool.tensor_tensor(out=x_sb[:, 2 * b + i, :], in0=x_sb[:, 2 * b + i, :], in1=a_sb[:, i, :],
                                       op=ALU.add).then_inc(xa_rdy, 1)

            def shared_hidden(b):
                for i in range(2):
                    n = 2 * b + i
                    pool.wait_ge(sgu_ev, n + 1)
                    if n >= 2:
                        pool.wait_ge(sht_mm, n - 1)
                    link(pool.tensor_tensor(out=h_sb[:, i, :], in0=gu_cp[:, i, 0:I], in1=sg_sb[:, i, :], op=ALU.mult))
                    pool.tensor_tensor(out=h_sb[:, i, :], in0=h_sb[:, i, :], in1=gu_cp[:, i, I:GU], op=ALU.mult).then_inc(sh_rdy, 1)

            pool.wait_ge(pre_rdy, NJ)
            add_attention(0)
            for b in range(NB):
                pool.wait_ge(st2_rdy, b + 1)
                rstd(r2, mv2[:, :, 0], mv2[:, :, 1], 2)
                for i in range(2):
                    if b > 1:
                        pool.wait_ge(xnt_mm, 2 * b - 3 + i)
                        pool.wait_ge(d_rows[b % 2][i], 16 * (b // 2))
                    pool.tensor_scalar(xn_of[b % 2][:, i, :], x_sb[:, 2 * b + i, :], r2[:, 4, i:i + 1], r2[:, 1, i:i + 1],
                                       ALU.add, ALU.mult).then_inc(xn_rdy, 1)
                if b + 1 < NB:
                    scale_sigmoid(b + 1)
                if b:
                    add_shared(b - 1)
                if b + 1 < NB:
                    add_attention(b + 1)
                shared_hidden(b)
            oh = onehot.rearrange("p (j k) e -> p j k e", k=TOPK)
            part = xn_sb[:, :, :].rearrange("p i (j e) -> p i j e", e=E)

            def weighted(k, dst):
                return pool.tensor_tensor(out=dst, in0=oh[:, :, k, :], in1=rw[:, :, k:k + 1].to_broadcast([P, NJ, E]), op=ALU.mult)

            pool.wait_ge(rw_rdy, 1)
            pool.wait_ge(oh_rdy, 2)
            pool.wait_ge(xnt_mm, 2 * NB - 2)
            for i in range(2):
                pool.wait_ge(d_rows[0][i], 16 * (NB // 2))
            weighted(0, comb[:, :, :])
            weighted(1, part[:, 0])
            link(weighted(2, part[:, 1]))
            link(pool.tensor_tensor(out=comb[:, :, :], in0=comb[:, :, :], in1=part[:, 0], op=ALU.add))
            weighted(3, part[:, 0])
            link(pool.tensor_tensor(out=comb[:, :, :], in0=comb[:, :, :], in1=part[:, 1], op=ALU.add))
            pool.tensor_tensor(out=comb[:, :, :], in0=comb[:, :, :], in1=part[:, 0], op=ALU.add).then_inc(comb_rdy, 1)
            add_shared(NB - 1)

            def gather(rows, u):
                pool.indirect_dma_start(xg_sb[:, u, :], None, rows_dram,
                                        bass.IndirectOffsetOnAxis(ap=rows.bitcast(u32), axis=0)).then_inc(g_done[u], 16)

            pool.wait_ge(d_zero, 16 * (NJ + 1))
            pool.wait_ge(d_comb, 16)
            for i in range(2):
                for b in range(2):
                    pool.wait_ge(d_rows[b][i], 16 * (NB // 2))
            pool.wait_ge(d_acc[0], 32 * (NB - 1))
            pool.wait_ge(slots_rdy, 1)
            for t in range(LEAD + 2):
                if t >= UNROLL:
                    pool.wait_ge(t_mm, t - UNROLL + 1)
                    pool.wait_ge(w_rdy, t - UNROLL + 1)
                gather(slot_row[:, t:t + 1], t % UNROLL)
            pool.wait_ge(d_acc[1], 32)
            pool.wait_ge(tab_rdy, 1)
            groups = pool.value_load(groups_i[0:1, 1:2], min_val=1, max_val=GROUPS)
            with pool.Fori(0, GROUPS) as g:
                with pool.If(g < groups):
                    for k in range(UNROLL):
                        h, v = k // 2, (k + 5) % UNROLL
                        if k % 2 == 0:
                            pool.wait_ge(t_mm, g * UNROLL + k + 3)
                            pool.tensor_tensor(out=ring_row[:, h, :], in0=slot_row[:, bass.ds(g * UNROLL + k, 7)],
                                               in1=zero_i[:, :].to_broadcast([P, 7]), op=ALU.add).then_inc(row_cp, 1)
                        pool.wait_ge(t_mm, g * UNROLL + k + 2)
                        pool.wait_ge(w_rdy, g * UNROLL + k + 2)
                        pool.sem_inc(issued, 1)
                        pool.wait_ge(row_cp, 1)
                        gather(ring_row[:, h, 5 + k % 2:6 + k % 2], v)
                        pool.wait_ge(y_ev, g * UNROLL + k + 2)
                        pool.wait_ge(sc_done[k % 2], g * (8 * UNROLL) + 16 + 16 * (k // 2))
                        pool.sem_inc(issued, 1)
                        pool.wait_ge(row_cp, 1)
                        pool.indirect_dma_start(acc_dram[k % 2],
                                                bass.IndirectOffsetOnAxis(ap=ring_row[:, h, k % 2:k % 2 + 1].bitcast(u32), axis=0),
                                                y_sb[:, k % 2, :], None, compute_op=ALU.add).then_inc(sc_done[k % 2], 16)
                        if k % 2:
                            pool.sem_clear(row_cp)
            for u in range(UNROLL):
                pool.wait_ge(g_done[u], groups * 16 + (32 if u == 0 else 16))

        @block.scalar
        def _(act):

            def qk_copy(b):
                for m, dst in enumerate((qt_sb, kt_sb)):
                    act.wait_ge(qk_mm, 2 * b + 2)
                    act.activation(dst[:, b * N:(b + 1) * N], pk[4 + b][0:DC, m * N:(m + 1) * N], ACT.Copy).then_inc(qk_ev, 1)

            def sim_copy(b):
                for i in range(2):
                    act.wait_ge(sim_mm, 2 * b + i + 1)
                    if b > 1:
                        act.wait_ge(masked, 2 * b - 3 + i)
                    act.activation(s_sb[b % 2][:, i, :], pk[1 + i][:, 0:N], ACT.Copy).then_inc(sim_ev, 1)

            def sim_sigmoid(b):
                for i in range(2):
                    if b:
                        act.wait_ge(masked, 2 * b - 1 + i)
                    act.activation(sig_sb[:, i, :], pk[1 + i][:, 0:N], ACT.Sigmoid, scale=SIM_SCALE).then_inc(sig_ev, 1)

            def shared_out(b):
                for i in range(2):
                    n = 2 * b + i
                    act.wait_ge(sht_mm, n + 1)
                    act.activation(ht_sb[:, i, :], pk[6 + i][0:IC, 0:2 * P], ACT.Copy).then_inc(sht_ev, 1)
                for i in range(2):
                    n = 2 * b + i
                    act.wait_ge(sy_mm, n + 1)
                    act.activation(gu_cp[:, i, 0:H], pk[6 + i][:, 2 * P:2 * P + H], ACT.Copy).then_inc(sy_ev, 1)

            qk_copy(0)
            sim_copy(0)
            qk_copy(1)
            sim_sigmoid(0)
            act.wait_ge(l_gam, 16)
            act.activation(gam[:, 1:2], gam[:, 0:1], ACT.Sigmoid).then_inc(gam_rdy, 1)
            sim_copy(1)
            qk_copy(2)
            qk_copy(3)
            for b in range(NB):
                if b + 1 < NB:
                    sim_sigmoid(b + 1)
                if b + 2 < NB:
                    sim_copy(b + 2)
                if b:
                    shared_out(b - 1)
                for i in range(2):
                    n = 2 * b + i
                    act.wait_ge(xnt_mm, n + 1)
                    if n >= 2:
                        act.wait_ge(sgu_mm, n - 1)
                    act.activation(xt_sb[:, i, :], xnt_ps[i][:, 0:KH * P], ACT.Copy).then_inc(xnt_ev, 1)
                if b == 0:
                    act.wait_ge(d_zero, 16 * (NJ + 1))
                    for a in range(2):
                        act.wait_ge(sc_done[a], 16)
                for i in range(2):
                    n = 2 * b + i
                    act.wait_ge(sgu_mm, n + 1)
                    if n >= 2:
                        act.wait_ge(sacc, n - 1)
                    act.activation(sg_sb[:, i, :], pk[6 + i][:, 0:I], ACT.Sigmoid)
                    act.activation(gu_cp[:, i, :], pk[6 + i][:, 0:GU], ACT.Copy).then_inc(sgu_ev, 1)
            act.wait_ge(v_rdy, 1)
            act.activation(ex[:, :, :], ex[:, :, :], ACT.Exp).then_inc(ex_rdy, 1)

            def token_numbers(j0, j1):
                act.wait_ge(c_pool, 16)
                for j in range(j0, j1):
                    act.wait_ge(soh_rdy, j + 1)
                    tile = slot_oh[:, j * TOPK:(j + 1) * TOPK, :]
                    act.activation(tile, tile, ACT.Copy, scale=tok1[:, j:j + 1]).then_inc(tok_rdy, 1)

            token_numbers(0, 2)
            shared_out(NB - 1)
            token_numbers(2, NJ)
            act.preload_act_table(ACT.Silu)

            for t in range(2):
                act.wait_ge(g_mm, t + 1)
                act.activation(sg_sb[:, t, :], pk[2 + t][:, 0:I], ACT.Silu).then_inc(g_silu, 1)
            act.wait_ge(ht_mm, 1)
            act.activation(ht_sb[:, 0, :], pk[4][0:IC, 0:2 * P], ACT.Copy).then_inc(ht_ev, 1)
            act.sem_inc(y_ev, 1)
            groups = act.value_load(groups_i[0:1, 1:2], min_val=1, max_val=GROUPS)
            with act.Fori(0, GROUPS) as g:
                with act.If(g < groups):
                    for k in range(UNROLL):
                        act.wait_ge(g_mm, g * UNROLL + k + 3)
                        act.wait_ge(h_rdy, g * UNROLL + k + 1)
                        act.activation(sg_sb[:, k % 2, :], pk[2 + k % 2][:, 0:I], ACT.Silu).then_inc(g_silu, 1)
                        act.wait_ge(ht_mm, g * UNROLL + k + 2)
                        act.activation(ht_sb[:, (k + 1) % 2, :], pk[4 + (k + 1) % 2][0:IC, 0:2 * P], ACT.Copy).then_inc(ht_ev, 1)
                        act.wait_ge(y_mm, g * UNROLL + k + 1)
                        act.wait_ge(w_rdy, g * UNROLL + k + 1)
                        if k < 2:
                            act.wait_ge(sc_done[k % 2], g * (8 * UNROLL) + 16)
                        else:
                            act.wait_ge(sc_done[k % 2], g * (8 * UNROLL) + 32)
                        act.activation(y_sb[:, k % 2, :], pk[6 + k % 2][:, 0:H], ACT.Copy, scale=wslot[:, k:k + 1]).then_inc(y_ev, 1)

        @block.vector
        def _(dve):
            for j in range(NJ):
                if j % (NJ // 2) == 0:
                    dve.wait_ge(l_x[j // (NJ // 2)], 16)
                last = dve.bn_stats(st1[:, j, :], x_sb[:, j, :])
            last.then_inc(dve_ch, 1)
            dve.wait_ge(dve_ch, 1)
            for j in range(NJ):
                last = dve.bn_aggr(mv1[:, j, :], st1[:, j, :])
            last.then_inc(st1_rdy, 1)
            chain = [1]
            count = [0, 0]

            def link(ins):
                chain[0] += 1
                ins.then_inc(dve_ch, 1)
                dve.wait_ge(dve_ch, chain[0])

            def step(i, make):
                if count[i]:
                    dve.wait_ge(chain_k[i], count[i])
                count[i] += 1
                make().then_inc(chain_k[i], 1)

            def x1(b):
                dve.wait_ge(at_mm, b + 1)
                dve.wait_ge(xa_rdy, 2 * b + 2)
                dve.wait_ge(c_pool, 16)
                for i in range(2):
                    j = 2 * b + i
                    last = dve.tensor_tensor(out=x_sb[:, j, :], in0=pk[3][:, i * N:(i + 1) * N], in1=x_sb[:, j, :], op=ALU.add)
                chain[0] += 1
                last.then_inc(dve_ch, 1)
                dve.wait_ge(dve_ch, chain[0])
                if b:
                    dve.wait_ge(xn_rdy, 2 * b)
                for i in range(2):
                    last = dve.bn_stats(st2[:, i, :], x_sb[:, 2 * b + i, :])
                link(last)
                for i in range(2):
                    last = dve.bn_aggr(mv2[:, i, :], st2[:, i, :])
                last.then_inc(st2_rdy, 1)

            def router(b):
                dve.wait_ge(lg_mm, 2 * b + 2)
                dve.wait_ge(l_rt, 32)
                chain[0] += 1
                dve.tensor_tensor(out=lg_sb[:, :, :], in0=pk[5][:, 0:2 * E].rearrange("p (i e) -> p i e", i=2),
                                  in1=rb_sb[:, :].rearrange("p (o e) -> p o e", o=1).to_broadcast([P, 2, E]),
                                  op=ALU.add).then_inc(dve_ch, 1)
                dve.wait_ge(dve_ch, chain[0])
                for i in range(2):
                    last = dve.max(v8[:, 2 * b + i, :], lg_sb[:, i, :])
                chain[0] += 1
                last.then_inc(dve_ch, 1)
                dve.wait_ge(dve_ch, chain[0])
                for i in range(2):
                    last = dve.max_index(i8[:, 2 * b + i, :], v8[:, 2 * b + i, :], lg_sb[:, i, :])
                last.then_inc(lg_ev, 1)

            full = (KTH - 1) // 8
            for b in range(NB):
                for r in range(full + 1):
                    for i in range(2):
                        if r == 0:
                            dve.wait_ge(sim_ev, 2 * b + i + 1)
                            if b:
                                dve.wait_ge(masked, 2 * b - 1 + i)
                            src = s_sb[b % 2][:, i, :]
                        else:
                            src = work_sb[:, i, :]
                        step(i, lambda: dve.max(m8[:, i, :], src))
                    if r < full:
                        for i in range(2):
                            src = s_sb[b % 2][:, i, :] if r == 0 else work_sb[:, i, :]
                            step(i, lambda: dve.match_replace(out=work_sb[:, i, :], in_to_replace=m8[:, i, :],
                                                              in_values=src, imm_value=NEG))
                    if b and r == 3:
                        x1(b - 1)
                    if b and r == 9:
                        router(b - 1)
                kth = (KTH - 1) % 8
                for i in range(2):
                    dve.wait_ge(chain_k[i], count[i])
                    dve.wait_ge(sig_rdy, 2 * b + i + 1)
                    if b:
                        dve.wait_ge(at_mm, b)
                        dve.wait_ge(xa_rdy, 2 * b)
                    dve.scalar_tensor_tensor(out=a_sb[:, i, :], in0=s_sb[b % 2][:, i, :], scalar=m8[:, i, kth:kth + 1],
                                             in1=sig_sb[:, i, :], op0=ALU.is_ge, op1=ALU.mult).then_inc(masked, 1)
            def one_hots(j0, j1):
                n = j1 - j0
                link(dve.tensor_copy(idx_f[:, j0:j1, :], i8[:, j0:j1, 0:TOPK]))
                iota_b = iota_f[:, 0:E].rearrange("p (o e) -> p o e", o=1).to_broadcast([P, n * TOPK, E])
                idx_b = idx_f[:, j0:j1, :].rearrange("p j k -> p (j k)").rearrange("p (c o) -> p c o", o=1).to_broadcast([P, n * TOPK, E])
                dve.tensor_tensor(out=onehot[:, j0 * TOPK:j1 * TOPK, :], in0=iota_b, in1=idx_b, op=ALU.is_equal).then_inc(oh_rdy, 1)

            def ranks(j0, j1, rank_ps):
                n, c0, c1 = j1 - j0, j0 * TOPK, j1 * TOPK
                rank_b = rank_ps.rearrange("p (j o e) -> p j o e", o=1, e=E).to_broadcast([P, n, TOPK, E])
                link(dve.tensor_tensor(out=prod[:, c0:c1, :].rearrange("p (j k) e -> p j k e", k=TOPK),
                                       in0=onehot[:, c0:c1, :].rearrange("p (j k) e -> p j k e", k=TOPK), in1=rank_b, op=ALU.mult))
                link(dve.reduce_sum(sl_f[:, c0:c1], prod[:, c0:c1, :], axis=AX))
                link(dve.tensor_copy(sl_i[:, 0, c0:c1], sl_f[:, c0:c1]))
                dve.tensor_scalar(sl_i[:, 1, c0:c1], sl_i[:, 0, c0:c1], P - 1, None, ALU.bitwise_and)
                link(dve.tensor_scalar(sl_i[:, 2, c0:c1], sl_i[:, 0, c0:c1], 7, None, ALU.logical_shift_right))
                link(dve.tensor_copy(sl_p[:, :, c0:c1], sl_i[:, 1:3, c0:c1]))

            def slot_one_hots(c0, c1):
                for c in range(c0, c1):
                    last = dve.tensor_scalar(slot_oh[:, c, :], iota_h[:, :], sl_p[:, 0, c:c + 1], None, ALU.is_equal)
                    if c % TOPK == TOPK - 1:
                        last.then_inc(soh_rdy, 1)

            dve.wait_ge(lg_ev, NB - 1)
            one_hots(0, EARLY)
            dve.wait_ge(masked, 2 * NB)
            x1(NB - 1)
            dve.wait_ge(rank_mm, 1)
            ranks(0, EARLY, pk[1][:, 0:EARLY * E])
            slot_one_hots(0, 16)
            router(NB - 1)
            dve.wait_ge(lg_ev, NB)
            one_hots(EARLY, NJ)
            dve.tensor_tensor(out=ex[:, :, :], in0=v8[:, :, 0:TOPK], in1=v8[:, :, 0:1].to_broadcast([P, NJ, TOPK]),
                              op=ALU.subtract).then_inc(v_rdy, 1)
            slot_one_hots(16, EARLY * TOPK)
            dve.wait_ge(rank_mm, 2)
            late_ps = pk[2][:, 0:(NJ - EARLY + 1) * E]
            link(dve.tensor_scalar(cnt_i[:, 0, :], late_ps[:, (NJ - EARLY) * E:], float(P - 1), None, ALU.add))
            link(dve.tensor_scalar(cnt_i[:, 1, :], cnt_i[:, 0, :], 7, None, ALU.logical_shift_right))
            link(dve.tensor_copy(ntl[:, 0, :], cnt_i[:, 1, :]))
            link(dve.tensor_tensor_scan(ntl[:, 1, :], ones_f[:, :], ntl[:, 0, :], 0.0, ALU.mult, ALU.add))
            link(dve.tensor_tensor(out=first_h, in0=ntl[:, 1, :], in1=ntl[:, 0, :], op=ALU.subtract))
            ranks(EARLY, NJ, late_ps[:, 0:(NJ - EARLY) * E])
            dve.wait_ge(ex_rdy, 1)
            link(dve.reduce_sum(sm[:, 0, :], ex[:, :, :], axis=AX))
            link(dve.reciprocal(sm[:, 1, :], sm[:, 0, :]))
            link(dve.tensor_scalar(sm[:, 2, :], sm[:, 1, :], ROUTE_SCALE, None, ALU.mult))
            dve.tensor_tensor(out=rw[:, :, :], in0=ex[:, :, :],
                              in1=sm[:, 2, :].rearrange("p (j o) -> p j o", o=1).to_broadcast([P, NJ, TOPK]), op=ALU.mult).then_inc(rw_rdy, 1)
            first_b = first_h.rearrange("p (o e) -> p o e", o=1).to_broadcast([P, NJ * TOPK, E])
            link(dve.tensor_tensor(out=prod_h, in0=onehot, in1=first_b, op=ALU.mult))
            link(dve.reduce_sum(sl_f[:, :], prod_h, axis=AX))
            link(dve.tensor_tensor(out=sl_p[:, 1, :], in0=sl_p[:, 1, :], in1=sl_f[:, :], op=ALU.add))
            slot_one_hots(EARLY * TOPK, NJ * TOPK)
            for c in range(NJ * TOPK):
                last = dve.tensor_scalar(tile_oh[:, c, :], iota_h[:, 0:NCOL], sl_p[:, 1, c:c + 1], None, ALU.is_equal)
                if c % 8 == 7:
                    last.then_inc(toh_rdy, 1)
            link(dve.tensor_scalar(srank[:, 0, :], ntl[:, 1, :], pidx[:, 0:1], 0.0, ALU.is_le, ALU.add, accum_out=ecol[:, :]))
            dve.tensor_scalar(ediag[:, :], ident[:, 0:NCOL], ecol[:, 0:1], None, ALU.mult).then_inc(ed_rdy, 1)
            link(dve.tensor_scalar(groups_i[:, 0:1], ntl[:, 1, E - 1:E], float(UNROLL - 1), None, ALU.add))
            dve.tensor_scalar(groups_i[:, 1:2], groups_i[:, 0:1], 2, None, ALU.logical_shift_right)
            dve.wait_ge(tab_mm, 1)
            link(dve.tensor_scalar(tmp_t[:, :], pk[3][:, 0:NCOL], 0.0, pad_row[:, 0:1], ALU.is_equal, ALU.mult))
            dve.scalar_tensor_tensor(out=slot_row[:, :], in0=pk[3][:, 0:NCOL], scalar=-1.0, in1=tmp_t[:, :],
                                     op0=ALU.add, op1=ALU.add).then_inc(slots_rdy, 1)
            dve.wait_ge(et_mm, 1)
            dve.tensor_copy(etile[:, :], pk[5][:, 0:NCOL])
            dve.tensor_scalar(etile_i[:, :], pk[5][:, 0:NCOL], float(E - 1), None, ALU.min).then_inc(tab_rdy, 1)

            def weights_of(expert_col, u):
                dve.scalar_tensor_tensor(out=srank[:, u, :], in0=iota_f[:, 0:E], scalar=expert_col,
                                         in1=xg_sb[:, u, H:XW], op0=ALU.is_equal, op1=ALU.mult,
                                         accum_out=wslot[:, u:u + 1]).then_inc(w_rdy, 1)

            def rows_out(k):
                dve.tensor_copy(xt_sb[:, k % 2, :], pk[k % 2][:, 0:KH * P]).then_inc(t_ev, 1)

            def gated(k):
                dve.tensor_tensor(out=h_sb[:, k % 2, :], in0=pk[2 + k % 2][:, I:GU], in1=sg_sb[:, k % 2, :],
                                  op=ALU.mult).then_inc(h_rdy, 1)

            dve.wait_ge(tab_rdy, 1)
            dve.wait_ge(sgu_mm, 2 * NB)
            dve.wait_ge(sht_mm, 2 * NB)
            groups = dve.value_load(groups_i[0:1, 1:2], min_val=1, max_val=GROUPS)
            for t in range(3):
                dve.wait_ge(t_mm, t + 1)
                rows_out(t)
                if t:
                    dve.wait_ge(g_silu, t)
                    gated(t - 1)
                dve.wait_ge(g_done[t], 16)
                weights_of(etile[:, t:t + 1], t)
            with dve.Fori(0, GROUPS) as g:
                with dve.If(g < groups):
                    for k in range(UNROLL):
                        u = (k + 3) % UNROLL
                        dve.wait_ge(t_mm, g * UNROLL + k + 4)
                        rows_out(k + 1)
                        dve.wait_ge(g_silu, g * UNROLL + k + 3)
                        dve.wait_ge(ht_mm, g * UNROLL + k + 1)
                        gated(k)
                        dve.wait_ge(g_done[u], g * 16 + 16 * ((k + 3) // UNROLL + 1))
                        dve.wait_ge(y_ev, g * UNROLL + k + 1)
                        weights_of(etile[:, bass.ds(g * UNROLL + k + 3, 1)], u)
            for b in range(NB):
                dve.wait_ge(f_ld[b], 32)
                dve.tensor_tensor(out=fin[:, 0, 2 * b:2 * b + 2, :], in0=fin[:, 0, 2 * b:2 * b + 2, :],
                                  in1=fin[:, 1, 2 * b:2 * b + 2, :], op=ALU.add).then_inc(f_add, 1)

        @block.tensor
        def _(pe):
            pe.wait_ge(l_ctx, 16)

            def qk(b):
                for m in range(2):
                    pe.matmul(pk[4 + b][0:DC, m * N:(m + 1) * N], wqk_sb[:, m * DC:(m + 1) * DC], ctx_sb[:, b * N:(b + 1) * N],
                              start=True, stop=True).then_inc(qk_mm, 1)

            def sims(b):
                pe.wait_ge(qk_ev, 2 * b + 2)
                for i in range(2):
                    if b:
                        pe.wait_ge(sig_ev, 2 * b - 1 + i)
                    r0 = (2 * b + i) * P
                    pe.matmul(pk[1 + i][:, 0:N], qt_sb[:, r0:r0 + P], kt_sb[:, b * N:(b + 1) * N],
                              start=True, stop=True).then_inc(sim_mm, 1)

            def shared_out(b):
                for i in range(2):
                    pe.wait_ge(sh_rdy, 2 * b + i + 1)
                    pe.wait_ge(sgu_ev, 2 * b + i + 1)
                    for c in range(2):
                        last = pe.transpose(pk[6 + i][0:IC, c * P:(c + 1) * P], h_sb[:, i, c * IC:(c + 1) * IC], ident[:, :])
                    last.then_inc(sht_mm, 1)
                for i in range(2):
                    n = 2 * b + i
                    pe.wait_ge(sht_ev, n + 1)
                    for c in range(2):
                        last = pe.matmul(pk[6 + i][:, 2 * P:2 * P + H], ht_sb[:, i, c * P:(c + 1) * P], wsd_sb[:, c * H:(c + 1) * H],
                                         start=c == 0, stop=c == 1)
                    last.then_inc(sy_mm, 1)

            oh = onehot.rearrange("p (j k) e -> p j k e", k=TOPK)

            def ranks_early():
                pe.wait_ge(oh_rdy, 1)
                pe.wait_ge(sig_ev, 2 * NB)
                for k in range(TOPK):
                    pe.matmul(pk[1][:, 0:EARLY * E], before_h[:, :], oh[:, 0:EARLY, k, :], start=k == 0, stop=False, skip_group_check=True)
                for j in range(EARLY - 1):
                    for k in range(TOPK):
                        last = pe.matmul(pk[1][:, (j + 1) * E:EARLY * E].rearrange("p (m e) -> p m e", e=E), ones_h[:, :],
                                         oh[:, j:j + 1, k, :].to_broadcast([P, EARLY - 1 - j, E]), start=False,
                                         stop=(j == EARLY - 2 and k == TOPK - 1), skip_group_check=True)
                last.then_inc(rank_mm, 1)
                for j in range(EARLY):
                    for k in range(TOPK):
                        pe.matmul(pk[2][:, 0:(NJ - EARLY + 1) * E].rearrange("p (m e) -> p m e", e=E), ones_h[:, :],
                                  oh[:, j:j + 1, k, :].to_broadcast([P, NJ - EARLY + 1, E]), start=(j == 0 and k == 0), stop=False,
                                  skip_group_check=True)

            def ranks_late():
                pe.wait_ge(oh_rdy, 2)
                late = NJ - EARLY
                for k in range(TOPK):
                    pe.matmul(pk[2][:, 0:late * E], before_h[:, :], oh[:, EARLY:NJ, k, :], start=False, stop=False, skip_group_check=True)
                for j in range(late):
                    for k in range(TOPK):
                        last = pe.matmul(pk[2][:, (j + 1) * E:(late + 1) * E].rearrange("p (m e) -> p m e", e=E), ones_h[:, :],
                                         oh[:, EARLY + j:EARLY + j + 1, k, :].to_broadcast([P, late - j, E]), start=False,
                                         stop=(j == late - 1 and k == TOPK - 1), skip_group_check=True)
                last.then_inc(rank_mm, 1)

            def transpose_a(b):
                pe.wait_ge(masked, 2 * b + 2)
                if b:
                    pe.wait_ge(st2_rdy, b)
                for i in range(2):
                    for c in range(2):
                        last = pe.transpose(pk[3][:, i * N + c * P:i * N + (c + 1) * P], a_sb[:, c, i * P:(i + 1) * P], ident[:, :])
                last.then_inc(at_mm, 1)

            qk(0)
            sims(0)
            qk(1)
            sims(1)
            qk(2)
            qk(3)
            pe.wait_ge(c_pool, 16)
            transpose_a(0)
            for b in range(NB):
                if b + 2 < NB:
                    sims(b + 2)
                if b == NB - 1:
                    ranks_early()
                if b:
                    shared_out(b - 1)
                for i in range(2):
                    n = 2 * b + i
                    pe.wait_ge(xn_rdy, n + 1)
                    if b:
                        pe.wait_ge(xnt_ev, n - 1)
                    for c in range(KH):
                        last = pe.transpose(xnt_ps[i][:, c * P:(c + 1) * P], xn_of[b % 2][:, i, c * P:(c + 1) * P], ident[:, :])
                    last.then_inc(xnt_mm, 1)
                if b:
                    pe.wait_ge(lg_ev, b)
                pe.wait_ge(l_rt, 32)
                for i in range(2):
                    pe.wait_ge(xnt_ev, 2 * b + i + 1)
                    for c in range(KH):
                        last = pe.matmul(pk[5][:, i * E:(i + 1) * E], xt_sb[:, i, c * P:(c + 1) * P], rw_sb[:, c * E:(c + 1) * E],
                                         start=c == 0, stop=c == KH - 1)
                    last.then_inc(lg_mm, 1)
                pe.wait_ge(l_ws, 32)
                for i in range(2):
                    n = 2 * b + i
                    if i and b + 1 < NB:
                        transpose_a(b + 1)
                    if n == NJ - 1:
                        ranks_late()
                    if b:
                        pe.wait_ge(sy_ev, n - 1)
                    for c in range(KH):
                        last = pe.matmul(pk[6 + i][:, 0:GU], xt_sb[:, i, c * P:(c + 1) * P], wsgu_sb[:, c * GU:(c + 1) * GU],
                                         start=c == 0, stop=c == KH - 1)
                    last.then_inc(sgu_mm, 1)
            shared_out(NB - 1)
            for c in range(NJ * TOPK):
                if c % 8 == 0:
                    pe.wait_ge(tok_rdy, c // TOPK + 2)
                    pe.wait_ge(toh_rdy, c // 8 + 1)
                last = pe.matmul(pk[3][:, 0:NCOL], slot_oh[:, c, :], tile_oh[:, c, :], start=c == 0, stop=c == NJ * TOPK - 1)
            last.then_inc(tab_mm, 1)
            pe.wait_ge(ed_rdy, 1)
            pe.matmul(pk[5][:, 0:NCOL], ones_h[:, :], ediag[:, :], start=True, stop=True).then_inc(et_mm, 1)
            for _ in range(2):
                pe.matmul(pk[4][:, :], ident[:, :], wsgu_sb[:, 0:512], start=True, stop=True)
            for s in l_w:
                pe.wait_ge(s, 16)

            def rows_t(k, u):
                for c in range(KH):
                    last = pe.transpose(pk[k % 2][:, c * P:(c + 1) * P], xg_sb[:, u, c * P:(c + 1) * P], ident[:, :])
                last.then_inc(t_mm, 1)

            def gate_up(k, e):
                for c in range(KH):
                    last = pe.matmul(pk[2 + k % 2][:, 0:GU], xt_sb[:, k % 2, c * P:(c + 1) * P],
                                     wgu_sb[:, bass.ds(e, 1), c * GU:(c + 1) * GU], start=c == 0, stop=c == KH - 1)
                last.then_inc(g_mm, 1)

            def h_t(k):
                for c in range(2):
                    last = pe.transpose(pk[4 + k % 2][0:IC, c * P:(c + 1) * P], h_sb[:, k % 2, c * IC:(c + 1) * IC], ident[:, :])
                last.then_inc(ht_mm, 1)

            def down(k, e):
                for c in range(2):
                    last = pe.matmul(pk[6 + k % 2][:, 0:H], ht_sb[:, k % 2, c * P:(c + 1) * P],
                                     wd_sb[:, bass.ds(e, 1), c * H:(c + 1) * H], start=c == 0, stop=c == 1)
                last.then_inc(y_mm, 1)

            def expert(t):
                return pe.value_load(etile_i[0:1, t:t + 1] if isinstance(t, int) else etile_i[0:1, bass.ds(t, 1)], min_val=0, max_val=E - 1)

            pe.wait_ge(tab_rdy, 1)
            pe.wait_ge(sy_ev, 2 * NB)
            groups = pe.value_load(groups_i[0:1, 1:2], min_val=1, max_val=GROUPS)
            e_first = [expert(t) for t in range(2)]
            pe.wait_ge(g_done[0], 16)
            rows_t(0, 0)
            for t in range(2):
                e_up = e_first[t]
                pe.wait_ge(t_ev, t + 1)
                gate_up(t, e_up)
                pe.wait_ge(g_done[t + 1], 16)
                rows_t(t + 1, t + 1)
            pe.wait_ge(h_rdy, 1)
            h_t(0)
            with pe.Fori(0, GROUPS) as g:
                with pe.If(g < groups):
                    for k in range(UNROLL):
                        u = (k + 3) % UNROLL
                        e_up, e_down = expert(g * UNROLL + k + 2), expert(g * UNROLL + k)
                        pe.wait_ge(t_ev, g * UNROLL + k + 3)
                        pe.wait_ge(h_rdy, g * UNROLL + k + 1)
                        gate_up(k, e_up)
                        pe.wait_ge(g_done[u], g * 16 + 16 * ((k + 3) // UNROLL + 1))
                        rows_t(k + 1, u)
                        pe.wait_ge(h_rdy, g * UNROLL + k + 2)
                        pe.wait_ge(ht_ev, g * UNROLL + max(k, 1))
                        h_t(k + 1)
                        pe.wait_ge(ht_ev, g * UNROLL + k + 1)
                        pe.wait_ge(y_ev, g * UNROLL + max(k, 1))
                        down(k, e_down)
            pe.sem_inc(experts_end, 1)


def kernel(x, ctx_512, L0_xattn_Wq, L0_xattn_Wk, L0_xattn_gamma_raw, L0_ffn_router_w, L0_ffn_router_b,
           L0_ffn_gate_w, L0_ffn_up_w, L0_ffn_down_w, L0_ffn_shared_gate_w, L0_ffn_shared_up_w, L0_ffn_shared_down_w):
    import numpy as np
    import concourse.bacc as bacc
    from concourse import mybir as mb
    from concourse.bass_utils import run_bass_kernel_spmd

    def chunks(w, k):
        return np.ascontiguousarray(w.T.reshape(-1, k, w.shape[0]).transpose(1, 0, 2).reshape(k, -1))

    gu = np.concatenate([np.asarray(L0_ffn_gate_w), np.asarray(L0_ffn_up_w)], axis=1)
    gu = gu.transpose(2, 0, 1).reshape(KH, P, E, GU).transpose(1, 2, 0, 3).reshape(P, E, KH * GU)
    dn = np.asarray(L0_ffn_down_w).transpose(2, 0, 1).reshape(2, IC, E, H).transpose(1, 2, 0, 3).reshape(IC, E, 2 * H)
    arrays = {
        "x_dram": np.asarray(x).reshape(TOK, H),
        "ctx_wqk_dram": np.concatenate([np.asarray(ctx_512).reshape(TOK, DC).T, np.asarray(L0_xattn_Wq).T,
                                        np.asarray(L0_xattn_Wk).T], axis=1),
        "gamma_dram": np.asarray(L0_xattn_gamma_raw).reshape(1, 1),
        "router_w_dram": chunks(np.asarray(L0_ffn_router_w), P),
        "router_b_dram": np.asarray(L0_ffn_router_b).reshape(1, E),
        "w_gu_dram": gu,
        "w_down_dram": dn,
        "ws_gu_dram": chunks(np.concatenate([np.asarray(L0_ffn_shared_gate_w), np.asarray(L0_ffn_shared_up_w)], axis=0), P),
        "ws_down_dram": chunks(np.asarray(L0_ffn_shared_down_w), IC),
    }
    arrays = {n: np.ascontiguousarray(a) for n, a in arrays.items()}
    nc = bacc.Bacc("TRN2", target_bir_lowering=False, num_devices=1, dynamic_dma_scratch_size=8192)
    args = [nc.dram_tensor(n, a.shape, mb.dt.from_np(a.dtype), kind="ExternalInput").ap() for n, a in arrays.items()]
    out = nc.dram_tensor("out_dram", (TOK, H), mb.dt.float32, kind="ExternalOutput").ap()
    build(nc, *args, out)
    r = run_bass_kernel_spmd(nc, [arrays], core_ids=[0])
    return r.results[0]["out_dram"].reshape(NB, N, H)
```

```python
import concourse.bass as bass
from concourse import mybir
from contextlib import ExitStack

P = 128
NB, N, H, DC = 4, 256, 256, 64
TOK = NB * N
NJ = TOK // P
E, I, TOPK = 32, 192, 4
KTH = int(N * 0.3)
EPS = 1e-5
ROUTE_SCALE = 1.8
SIM_SCALE = 1.0 / 16.0
KH = H // P
IC = I // 2
GU = 2 * I
XW = H + 2 * TOPK
MAX_TILES = E + (TOK * TOPK - E) // P
MIN_TILES = TOK * TOPK // P
UNROLL = 4
FIRST_GATHERS = UNROLL + 1
GROUPS = -(-(MAX_TILES - 1) // UNROLL)
EARLY = (NB - 1) * 2
NCOL = 72
assert NCOL >= MAX_TILES + 4 and NCOL % 4 == 0
ROWS = TOK + P
NEG = -3.0e38
OHG = 8
WGRP = 4
FINAL = (((0, 4), (4, 8)), ((0, 2), (2, 4), (4, 6), (6, 7), (7, 8)))


def build(nc, x, ctx_wqk, gamma, router_w, router_b, w_gu, w_down, ws_gu, ws_down, out):
    f32, f16 = mybir.dt.float32, mybir.dt.float16
    i32, u32 = mybir.dt.int32, mybir.dt.uint32
    ALU = mybir.AluOpType
    ACT = mybir.ActivationFunctionType
    AX = mybir.AxisListType.X

    rows_dram = nc.dram_tensor("token_rows", (ROWS, XW), f32, kind="Internal").ap()
    acc_dram = [nc.dram_tensor(f"acc{a}", (ROWS, H), f32, kind="Internal").ap() for a in range(2)]

    ctx = ExitStack()
    with ctx:
        def sb(name, shape, dt=f32):
            return ctx.enter_context(nc.sbuf_tensor(name, shape, dt))

        def sem(name):
            return ctx.enter_context(nc.semaphore(name))

        wgu_sb = sb("wgu_sb", [P, E, KH * GU])
        wd_sb = sb("wd_sb", [IC, E, 2 * H])
        wsgu_sb = sb("wsgu_sb", [P, KH * GU])
        wsd_sb = sb("wsd_sb", [IC, 2 * H])
        rw_sb = sb("rw_sb", [P, KH * E])
        rb_sb = sb("rb_sb", [1, E])
        x_sb = sb("x_sb", [P, NJ, H])
        xg_sb = x_sb[:, 0:5, :].rearrange("p j h -> p (j h)")[:, 0:4 * XW].rearrange("p (u w) -> p u w", u=4)
        arena = sb("arena", [P, 4736])
        cw_sb = arena[0:DC, 0:TOK + 2 * DC]
        ctx_sb, wqk_sb = cw_sb[:, 0:TOK], cw_sb[:, TOK:]
        qt_sb = arena[0:DC, 1152:2176]
        kt_sb = arena[0:DC, 2176:3200]
        s_sb = [wgu_sb[:, E - 1, 0:2 * N].rearrange("p (i n) -> p i n", i=2), arena[:, 3200:3712].rearrange("p (i n) -> p i n", i=2)]
        sig_sb = arena[:, 3712:4224].rearrange("p (i n) -> p i n", i=2)
        a_sb = arena[:, 4224:4736].rearrange("p (i n) -> p i n", i=2)
        onehot = arena[:, 0:512].bitcast(f16).rearrange("p (c e) -> p c e", e=E)
        prod = arena[:, 512:1536].rearrange("p (c e) -> p c e", e=E)
        prod_h = arena[:, 512:1024].bitcast(f16).rearrange("p (c e) -> p c e", e=E)
        slot_oh = arena[:, 1536:3584].bitcast(f16).rearrange("p (c s) -> p c s", s=P)
        tile_oh = arena[:, 3584:3584 + 16 * NCOL].bitcast(f16).rearrange("p (q t c) -> p q t c", t=NCOL, c=OHG)
        work_sb = sb("work_sb", [P, 2, N])
        xn_sb = sb("xn_sb", [P, 2, H])
        xt_sb = sb("xt_sb", [P, 2, KH * P])
        sg_sb = sb("sg_sb", [P, 2, I])
        h_sb = sb("h_sb", [P, 2, I])
        iota_i = h_sb[:, 0, 0:P].bitcast(i32)
        ht_sb = sb("ht_sb", [IC, 2, 2 * P])
        y_sb = sb("y_sb", [P, 2, H])
        xn_of = [xn_sb, y_sb]
        gu_cp = sb("gu_cp", [P, 2, GU])
        zero_sb = gu_cp[:, 1, 0:XW]
        ident = sb("ident", [P, P])
        ones_f = sb("ones_f", [P, P])
        ones_h = sb("ones_h", [P, P], f16)
        before_h = sb("before_h", [P, P], f16)
        iota_f = sb("iota_f", [P, P])
        iota_h = sb("iota_h", [P, P], f16)
        iota_rep = sb("iota_rep", [P, NCOL, OHG], f16)
        pidx_i = sb("pidx_i", [P, NJ], i32)
        tok1 = sb("tok1", [P, NJ])
        pad_row = sb("pad_row", [P, 1])
        pidx = sb("pidx", [P, 1])
        gam = sb("gam", [P, 4])
        st1 = sb("st1", [P, NJ, 6])
        mv1 = sb("mv1", [P, NJ, 2])
        r1 = sb("r1", [P, 6, NJ])
        half = sb("half", [P, 1])
        st2 = sb("st2", [P, 2, 6])
        mv2 = sb("mv2", [P, 2, 2])
        r2 = sb("r2", [P, 5, 2])
        m8 = sb("m8", [P, 2, 8])
        v8 = sb("v8", [P, NJ, 8])
        i8 = sb("i8", [P, NJ, 8], u32)
        iw_sb = sb("iw_sb", [P, NJ, 2 * TOPK])
        idx_f, rw = iw_sb[:, :, 0:TOPK], iw_sb[:, :, TOPK:]
        ex = sb("ex", [P, NJ, TOPK])
        sm = sb("sm", [P, 3, NJ])
        cnt_i = sb("cnt_i", [P, 2, E], i32)
        ntl = work_sb[:, 0, 0:4 * E].rearrange("p (n e) -> p n e", e=E)
        first_h = ntl[:, 2, 0:E // 2].bitcast(f16)
        srank = work_sb[:, 1, :].rearrange("p (j e) -> p j e", e=E)
        sl_f = sb("sl_f", [P, NJ * TOPK])
        sl_i = work_sb[:, 0, 4 * E:4 * E + 3 * NJ * TOPK].bitcast(i32).rearrange("p (n c) -> p n c", n=3)
        sl_t = sb("sl_t", [P, NJ * TOPK], f16)
        sl_p = sb("sl_p", [P, 2, NJ * TOPK])
        ecol = sb("ecol", [P, 1])
        ediag = sb("ediag", [P, NCOL], f16)
        etile = sb("etile", [P, NCOL])
        elow = sb("elow", [P, NCOL])
        etwo_i = sb("etwo_i", [P, NCOL - 2], i32)
        tmp_t = sb("tmp_t", [P, NCOL])
        slot_row = sb("slot_row", [P, NCOL], i32)
        ring_row = sb("ring_row", [P, 2, 7], i32)
        full_i = sb("full_i", [P, 1], i32)
        last_row = sb("last_row", [P, 2], i32)
        zero_i = sb("zero_i", [P, 1], i32)
        wslot = sb("wslot", [P, UNROLL])
        pk = [ctx.enter_context(nc.psum_tensor(f"pk{n}", [P, 512], f32)) for n in range(8)]

        xnt_ps = [pk[4], pk[0]]

        l_ctx, l_gam, l_rt, l_ws = sem("l_ctx"), sem("l_gam"), sem("l_rt"), sem("l_ws")
        l_x = [sem(f"l_x{hf}") for hf in range(2)]
        l_w = [sem(f"l_w{n}") for n in range(2 * E // WGRP)]
        c_pool, c_ready = sem("c_pool"), sem("c_ready")
        qk_mm, qk_ev = sem("qk_mm"), sem("qk_ev")
        sim_mm, sim_ev, sig_ev, sig_rdy, masked = sem("sim_mm"), sem("sim_ev"), sem("sig_ev"), sem("sig_rdy"), sem("masked")
        gam_rdy, st1_rdy, pre_rdy, pool_ch = sem("gam_rdy"), sem("st1_rdy"), sem("pre_rdy"), sem("pool_ch")
        chain_k = [sem(f"chain_k{i}") for i in range(5)]
        dve_ch = sem("dve_ch")
        at_mm, st2_rdy, xn_rdy = sem("at_mm"), sem("st2_rdy"), sem("xn_rdy")
        xnt_mm, xnt_ev, lg_mm, lg_ev = sem("xnt_mm"), sem("xnt_ev"), sem("lg_mm"), sem("lg_ev")
        sgu_mm, sgu_ev, sh_rdy, sht_mm, sht_ev = sem("sgu_mm"), sem("sgu_ev"), sem("sh_rdy"), sem("sht_mm"), sem("sht_ev")
        sy_mm, sy_ev, sacc, xa_rdy = sem("sy_mm"), sem("sy_ev"), sem("sacc"), sem("xa_rdy")
        d_rows = [[sem(f"d_rows{b}{i}") for i in range(2)] for b in range(2)]
        d_acc = [sem("d_acc"), sem("d_acc_last")]
        d_zero, d_choices = sem("d_zero"), sem("d_choices")
        v_rdy, ex_rdy, oh_rdy, rank_mm = sem("v_rdy"), sem("ex_rdy"), sem("oh_rdy"), sem("rank_mm")
        ed_rdy, et_mm, slots_rdy, rw_rdy, toh_rdy, tab_mm = (sem(n) for n in ("ed_rdy", "et_mm", "slots_rdy", "rw_rdy", "toh_rdy", "tab_mm"))
        tab_rdy, soh_rdy, tok_rdy = sem("tab_rdy"), sem("soh_rdy"), sem("tok_rdy")
        g_done = [sem(f"g_done{u}") for u in range(UNROLL)]
        row_cp = sem("row_cp")
        t_mm, t_ev, g_mm, g_silu, h_rdy = sem("t_mm"), sem("t_ev"), sem("g_mm"), sem("g_silu"), sem("h_rdy")
        ht_mm, ht_ev, y_mm, y_ev, w_rdy = sem("ht_mm"), sem("ht_ev"), sem("y_mm"), sem("y_ev"), sem("w_rdy")
        sc_done = [sem(f"sc_done{a}") for a in range(2)]
        issued = sem("issued")
        last_cp = sem("last_cp")
        f_ld = [[sem(f"f_ld{a}{c}") for c in range(len(FINAL[a]))] for a in range(2)]
        f_add, f_st = sem("f_add"), sem("f_st")

        fin = wgu_sb[:, 0:6, :].rearrange("p e w -> p (e w)")[:, 0:2 * NJ * H].rearrange("p (a j h) -> p a j h", a=2, j=NJ)

        block = ctx.enter_context(nc.Block())

        @block.sync
        def _(sp):
            sp.dma_start(cw_sb, ctx_wqk).then_inc(l_ctx, 16)
            for hf in range(2):
                j0 = hf * NJ // 2
                sp.dma_start(x_sb[:, j0:j0 + NJ // 2, :], x[j0 * P:(j0 + NJ // 2) * P, :].rearrange("(j p) h -> p j h", p=P)).then_inc(l_x[hf], 16)
            sp.dma_start(gam[:, 0:1], gamma.to_broadcast([P, 1])).then_inc(l_gam, 16)
            sp.dma_start(rw_sb[:, :], router_w).then_inc(l_rt, 16)
            sp.dma_start(rb_sb[:, :], router_b).then_inc(l_rt, 16)
            sp.wait_ge(c_ready, 1)
            sp.dma_start(rows_dram[TOK:ROWS, :], zero_sb).then_inc(d_zero, 16)
            for j in range(NJ):
                sp.dma_start(acc_dram[1][j * P:(j + 1) * P, :], gu_cp[:, 1, 0:H]).then_inc(d_zero, 16)
            sp.dma_start(wsgu_sb[:, :], ws_gu).then_inc(l_ws, 16)
            sp.dma_start(wsd_sb[:, :], ws_down).then_inc(l_ws, 16)

            def weights(n0, n1):
                for n in range(n0, n1):
                    e0 = n * WGRP
                    if n == E // WGRP - 1:
                        sp.wait_ge(masked, 2 * NB - 2)
                    sp.dma_start(wgu_sb[:, e0:e0 + WGRP, :], w_gu[:, e0:e0 + WGRP, :]).then_inc(l_w[2 * n], 16)
                    sp.dma_start(wd_sb[:, e0:e0 + WGRP, :], w_down[:, e0:e0 + WGRP, :]).then_inc(l_w[2 * n + 1], 16)

            def store_residual(b):
                for i in range(2):
                    n = 2 * b + i
                    sp.wait_ge(sacc, n + 1)
                    sp.dma_start(acc_dram[0][n * P:(n + 1) * P, :], x_sb[:, n, :]).then_inc(d_acc[b // (NB - 1)], 16)

            weight_groups = (2, 5, 7, 8, 8)
            weights(0, weight_groups[0])
            for b in range(NB):
                for i in range(2):
                    n = 2 * b + i
                    sp.wait_ge(xn_rdy, n + 1)
                    sp.dma_start(rows_dram[n * P:(n + 1) * P, 0:H], xn_of[b % 2][:, i, :]).then_inc(d_rows[b % 2][i], 16)
                weights(weight_groups[b], weight_groups[b + 1])
                if b:
                    store_residual(b - 1)
            sp.wait_ge(rw_rdy, 1)
            sp.dma_start(rows_dram[0:TOK, H:XW].rearrange("(j p) e -> p j e", p=P), iw_sb[:, :, :]).then_inc(d_choices, 16)
            store_residual(NB - 1)
            sp.wait_ge(tab_rdy, 1)
            full = sp.value_load(full_i[0:1, 0:1], min_val=MIN_TILES - 2, max_val=MAX_TILES - 2)
            sp.wait_ge(y_mm, full + 2)
            def pieces(t, c0, c1):
                return t[c0 * P:c1 * P, :].rearrange("(j p) h -> p j h", p=P)

            for a in range(2):
                sp.wait_ge(sc_done[a], ((full + (5 - a)) >> 1) * 16)
                for c, (j0, j1) in enumerate(FINAL[a]):
                    sp.dma_start(fin[:, a, j0:j1, :], pieces(acc_dram[a], j0, j1)).then_inc(f_ld[a][c], 16)
            for c, (j0, j1) in enumerate(FINAL[1]):
                sp.wait_ge(f_add, c + 1)
                sp.dma_start(pieces(out, j0, j1), fin[:, 0, j0:j1, :]).then_inc(f_st, 16)
            sp.wait_ge(f_st, 16 * len(FINAL[1]))

        @block.gpsimd
        def _(pool):
            pool.memset(zero_sb, 0.0).then_inc(c_ready, 1)
            pool.memset(half[:, :], -0.5).then_inc(c_pool, 1)
            pool.memset(ident[:, :], 0.0).then_inc(c_pool, 1)
            pool.memset(ones_h[:, :], 1.0).then_inc(c_pool, 1)
            pool.memset(ones_f[:, :], 1.0).then_inc(c_pool, 1)
            pool.memset(zero_i[:, :], 0).then_inc(c_pool, 1)
            pool.iota(iota_i, [[1, P]], base=0, channel_multiplier=0).then_inc(c_pool, 1)
            pool.iota(pidx_i[:, :], [[P, NJ]], base=0, channel_multiplier=1).then_inc(c_pool, 1)
            pool.wait_ge(c_ready, 1)
            for a in range(2):
                pool.dma_start(acc_dram[a][TOK:ROWS, :], gu_cp[:, 1, 0:H]).then_inc(sc_done[a], 16)
            pool.wait_ge(c_pool, 7)
            pool.affine_select(out=ident[:, :], in_=ident[:, :], compare_op=ALU.not_equal, fill=1.0, base=0,
                               pattern=[[-1, P]], channel_multiplier=1).then_inc(c_pool, 1)
            pool.affine_select(out=before_h[:, :], in_=ones_h[:, :], compare_op=ALU.is_gt, fill=0.0, base=0,
                               pattern=[[1, P]], channel_multiplier=-1).then_inc(c_pool, 1)
            pool.tensor_copy(iota_f[:, :], iota_i).then_inc(c_pool, 1)
            pool.tensor_copy(iota_h[:, :], iota_i).then_inc(c_pool, 1)
            pool.tensor_copy(pidx[:, :], pidx_i[:, 0:1]).then_inc(c_pool, 1)
            pool.tensor_scalar(tok1[:, :], pidx_i[:, :], 1.0, None, ALU.add).then_inc(c_pool, 1)
            pool.tensor_scalar(pad_row[:, :], pidx_i[:, 0:1], float(TOK + 1), None, ALU.add).then_inc(c_pool, 1)
            pool.wait_ge(gam_rdy, 1)
            pool.tensor_scalar(gam[:, 2:3], gam[:, 1:2], -1.0, 1.0, ALU.mult, ALU.add).then_inc(c_pool, 1)
            pool.tensor_scalar(gam[:, 3:4], gam[:, 1:2], 0.5, None, ALU.mult).then_inc(c_pool, 1)
            pool.wait_ge(c_pool, 16)
            pool.tensor_copy(iota_rep[:, :, :], iota_f[:, 0:NCOL].rearrange("p (t o) -> p t o", o=1).to_broadcast([P, NCOL, OHG])).then_inc(c_pool, 1)
            chain = [0]

            def link(ins):
                chain[0] += 1
                ins.then_inc(pool_ch, 1)
                pool.wait_ge(pool_ch, chain[0])

            def rstd(t, mean, var, n):
                link(pool.tensor_scalar(t[:, 0, :], var, EPS, None, ALU.add))
                pool.tensor_scalar(t[:, 4, :], mean, -1.0, None, ALU.mult)
                link(pool.tensor_tensor(out=t[:, 1, :], in0=t[:, 0, :], in1=half[:, 0:1].to_broadcast([P, n]), op=ALU.pow))
                link(pool.tensor_tensor(out=t[:, 2, :], in0=t[:, 1, :], in1=t[:, 1, :], op=ALU.mult))
                link(pool.tensor_tensor(out=t[:, 3, :], in0=t[:, 2, :], in1=t[:, 0, :], op=ALU.mult))
                link(pool.tensor_scalar(t[:, 2, :], t[:, 3, :], -0.5, 1.5, ALU.mult, ALU.add))
                link(pool.tensor_tensor(out=t[:, 1, :], in0=t[:, 1, :], in1=t[:, 2, :], op=ALU.mult))

            def scale_sigmoid(b):
                for i in range(2):
                    pool.wait_ge(sig_ev, 2 * b + i + 1)
                    pool.tensor_scalar(sig_sb[:, i, :], sig_sb[:, i, :], gam[:, 3:4], None, ALU.mult).then_inc(sig_rdy, 1)

            scale_sigmoid(0)
            pool.wait_ge(st1_rdy, 1)
            rstd(r1, mv1[:, :, 0], mv1[:, :, 1], NJ)
            link(pool.tensor_scalar(r1[:, 5, :], r1[:, 1, :], gam[:, 2:3], None, ALU.mult))
            link(pool.tensor_tensor(out=r1[:, 3, :], in0=r1[:, 5, :], in1=r1[:, 4, :], op=ALU.mult))
            link(pool.tensor_scalar(r1[:, 2, :], r1[:, 5, :], 1.0, None, ALU.add))
            for j in range(NJ):
                pool.tensor_scalar(x_sb[:, j, :], x_sb[:, j, :], r1[:, 2, j:j + 1], r1[:, 3, j:j + 1],
                                   ALU.mult, ALU.add).then_inc(pre_rdy, 1)

            def add_shared(b):
                for i in range(2):
                    n = 2 * b + i
                    pool.wait_ge(sy_ev, n + 1)
                    pool.tensor_tensor(out=x_sb[:, n, :], in0=x_sb[:, n, :], in1=gu_cp[:, i, 0:H], op=ALU.add).then_inc(sacc, 1)

            def add_attention(b):
                for i in range(2):
                    pool.wait_ge(masked, 2 * b + i + 1)
                    pool.tensor_tensor(out=x_sb[:, 2 * b + i, :], in0=x_sb[:, 2 * b + i, :], in1=a_sb[:, i, :],
                                       op=ALU.add).then_inc(xa_rdy, 1)

            def shared_hidden(b):
                for i in range(2):
                    n = 2 * b + i
                    pool.wait_ge(sgu_ev, n + 1)
                    if n >= 2:
                        pool.wait_ge(sht_mm, n - 1)
                    link(pool.tensor_tensor(out=h_sb[:, i, :], in0=gu_cp[:, i, 0:I], in1=sg_sb[:, i, :], op=ALU.mult))
                    pool.tensor_tensor(out=h_sb[:, i, :], in0=h_sb[:, i, :], in1=gu_cp[:, i, I:GU], op=ALU.mult).then_inc(sh_rdy, 1)

            pool.wait_ge(pre_rdy, NJ)
            add_attention(0)
            for b in range(NB):
                pool.wait_ge(st2_rdy, b + 1)
                rstd(r2, mv2[:, :, 0], mv2[:, :, 1], 2)
                for i in range(2):
                    if b > 1:
                        pool.wait_ge(xnt_mm, 2 * b - 3 + i)
                        pool.wait_ge(d_rows[b % 2][i], 16 * (b // 2))
                    pool.tensor_scalar(xn_of[b % 2][:, i, :], x_sb[:, 2 * b + i, :], r2[:, 4, i:i + 1], r2[:, 1, i:i + 1],
                                       ALU.add, ALU.mult).then_inc(xn_rdy, 1)
                if b + 1 < NB:
                    scale_sigmoid(b + 1)
                if b:
                    add_shared(b - 1)
                if b + 1 < NB:
                    add_attention(b + 1)
                shared_hidden(b)
            add_shared(NB - 1)

            def gather(rows, u):
                pool.indirect_dma_start(xg_sb[:, u, :], None, rows_dram,
                                        bass.IndirectOffsetOnAxis(ap=rows.bitcast(u32), axis=0)).then_inc(g_done[u], 16)

            pool.wait_ge(d_zero, 16 * (NJ + 1))
            pool.wait_ge(d_choices, 16)
            for i in range(2):
                for b in range(2):
                    pool.wait_ge(d_rows[b][i], 16 * (NB // 2))
            pool.wait_ge(d_acc[0], 32 * (NB - 1))
            pool.wait_ge(slots_rdy, 1)
            for t in range(FIRST_GATHERS):
                if t >= UNROLL:
                    pool.wait_ge(t_mm, t - UNROLL + 1)
                    pool.wait_ge(w_rdy, t - UNROLL + 1)
                gather(slot_row[:, t:t + 1], t % UNROLL)
            pool.wait_ge(d_acc[1], 32)
            pool.wait_ge(tab_rdy, 1)
            full = pool.value_load(full_i[0:1, 0:1], min_val=MIN_TILES - 2, max_val=MAX_TILES - 2)

            def slot(g, k):
                h, v = k // 2, (k + 5) % UNROLL
                if k % 2 == 0:
                    pool.wait_ge(t_mm, g * UNROLL + k + 3)
                    pool.tensor_tensor(out=ring_row[:, h, :], in0=slot_row[:, bass.ds(g * UNROLL + k, 7)],
                                       in1=zero_i[:, :].to_broadcast([P, 7]), op=ALU.add).then_inc(row_cp, 1)
                pool.wait_ge(t_mm, g * UNROLL + k + 2)
                pool.wait_ge(w_rdy, g * UNROLL + k + 2)
                pool.sem_inc(issued, 1)
                pool.wait_ge(row_cp, 1)
                gather(ring_row[:, h, 5 + k % 2:6 + k % 2], v)
                pool.wait_ge(y_ev, g * UNROLL + k + 2)
                pool.wait_ge(sc_done[k % 2], g * (8 * UNROLL) + 16 + 16 * (k // 2))
                pool.sem_inc(issued, 1)
                pool.wait_ge(row_cp, 1)
                pool.indirect_dma_start(acc_dram[k % 2],
                                        bass.IndirectOffsetOnAxis(ap=ring_row[:, h, k % 2:k % 2 + 1].bitcast(u32), axis=0),
                                        y_sb[:, k % 2, :], None, compute_op=ALU.add).then_inc(sc_done[k % 2], 16)
                if k % 2:
                    pool.sem_clear(row_cp)

            def last_two(k):
                pool.tensor_tensor(out=last_row[:, :], in0=slot_row[:, bass.ds(full, 2)],
                                   in1=zero_i[:, :].to_broadcast([P, 2]), op=ALU.add).then_inc(last_cp, 1)
                for i in range(2):
                    a = (k + i) % 2
                    pool.wait_ge(y_ev, full + (2 + i))
                    pool.wait_ge(sc_done[a], ((full + (2 + i)) >> 1) * 16)
                    pool.sem_inc(issued, 1)
                    pool.wait_ge(last_cp, 1)
                    pool.indirect_dma_start(acc_dram[a], bass.IndirectOffsetOnAxis(ap=last_row[:, i:i + 1].bitcast(u32), axis=0),
                                            y_sb[:, a, :], None, compute_op=ALU.add).then_inc(sc_done[a], 16)

            with pool.Fori(0, GROUPS) as g:
                with pool.If(g * UNROLL < full):
                    slot(g, 0)
                    with pool.If(g * UNROLL + 1 < full):
                        slot(g, 1)
                        with pool.If(g * UNROLL + 2 < full):
                            slot(g, 2)
                            with pool.If(g * UNROLL + 3 < full):
                                slot(g, 3)
                            with pool.Else():
                                last_two(3)
                        with pool.Else():
                            last_two(2)
                    with pool.Else():
                        last_two(1)
                with pool.Else():
                    with pool.If(g * UNROLL == full):
                        last_two(0)
            for u in range(UNROLL):
                pool.wait_ge(g_done[u], ((full + (8 - u)) >> 2) * 16)

        @block.scalar
        def _(act):

            def qk_copy(b):
                for m, dst in enumerate((qt_sb, kt_sb)):
                    act.wait_ge(qk_mm, 2 * b + 2)
                    act.activation(dst[:, b * N:(b + 1) * N], pk[4 + b][0:DC, m * N:(m + 1) * N], ACT.Copy).then_inc(qk_ev, 1)

            def sim_copy(b):
                for i in range(2):
                    act.wait_ge(sim_mm, 2 * b + i + 1)
                    if b > 1:
                        act.wait_ge(masked, 2 * b - 3 + i)
                    act.activation(s_sb[b % 2][:, i, :], pk[1 + i][:, 0:N], ACT.Copy).then_inc(sim_ev, 1)

            def sim_sigmoid(b):
                for i in range(2):
                    if b:
                        act.wait_ge(masked, 2 * b - 1 + i)
                    act.activation(sig_sb[:, i, :], pk[1 + i][:, 0:N], ACT.Sigmoid, scale=SIM_SCALE).then_inc(sig_ev, 1)

            def shared_out(b):
                for i in range(2):
                    n = 2 * b + i
                    act.wait_ge(sht_mm, n + 1)
                    act.activation(ht_sb[:, i, :], pk[6 + i][0:IC, 0:2 * P], ACT.Copy).then_inc(sht_ev, 1)
                for i in range(2):
                    n = 2 * b + i
                    act.wait_ge(sy_mm, n + 1)
                    act.activation(gu_cp[:, i, 0:H], pk[6 + i][:, 2 * P:2 * P + H], ACT.Copy).then_inc(sy_ev, 1)

            def token_numbers(j0, j1):
                act.wait_ge(c_pool, 16)
                for j in range(j0, j1):
                    act.wait_ge(soh_rdy, j + 1)
                    tile = slot_oh[:, j * TOPK:(j + 1) * TOPK, :]
                    act.activation(tile, tile, ACT.Copy, scale=tok1[:, j:j + 1]).then_inc(tok_rdy, 1)

            qk_copy(0)
            sim_copy(0)
            qk_copy(1)
            sim_sigmoid(0)
            act.wait_ge(l_gam, 16)
            act.activation(gam[:, 1:2], gam[:, 0:1], ACT.Sigmoid).then_inc(gam_rdy, 1)
            sim_copy(1)
            qk_copy(2)
            qk_copy(3)
            for b in range(NB):
                if b + 1 < NB:
                    sim_sigmoid(b + 1)
                if b + 2 < NB:
                    sim_copy(b + 2)
                if b:
                    shared_out(b - 1)
                for i in range(2):
                    n = 2 * b + i
                    act.wait_ge(xnt_mm, n + 1)
                    if n >= 2:
                        act.wait_ge(sgu_mm, n - 1)
                    act.activation(xt_sb[:, i, :], xnt_ps[i][:, 0:KH * P], ACT.Copy).then_inc(xnt_ev, 1)
                if b == NB - 1:
                    token_numbers(0, 2)
                if b == 0:
                    act.wait_ge(d_zero, 16 * (NJ + 1))
                    for a in range(2):
                        act.wait_ge(sc_done[a], 16)
                for i in range(2):
                    n = 2 * b + i
                    act.wait_ge(sgu_mm, n + 1)
                    if n >= 2:
                        act.wait_ge(sacc, n - 1)
                    act.activation(sg_sb[:, i, :], pk[6 + i][:, 0:I], ACT.Sigmoid)
                    act.activation(gu_cp[:, i, :], pk[6 + i][:, 0:GU], ACT.Copy).then_inc(sgu_ev, 1)
                    if n == NJ - 2:
                        token_numbers(2, 4)
            act.wait_ge(v_rdy, 1)
            act.activation(ex[:, :, :], ex[:, :, :], ACT.Exp).then_inc(ex_rdy, 1)

            shared_out(NB - 1)
            token_numbers(4, EARLY)
            act.preload_act_table(ACT.Silu)

            for t in range(2):
                act.wait_ge(g_mm, t + 1)
                act.activation(sg_sb[:, t, :], pk[2 + t][:, 0:I], ACT.Silu).then_inc(g_silu, 1)
            act.wait_ge(ht_mm, 1)
            act.activation(ht_sb[:, 0, :], pk[4][0:IC, 0:2 * P], ACT.Copy).then_inc(ht_ev, 1)
            act.sem_inc(y_ev, 1)
            full = act.value_load(full_i[0:1, 0:1], min_val=MIN_TILES - 2, max_val=MAX_TILES - 2)

            def slot(g, k):
                act.wait_ge(g_mm, g * UNROLL + k + 3)
                act.wait_ge(h_rdy, g * UNROLL + k + 1)
                act.activation(sg_sb[:, k % 2, :], pk[2 + k % 2][:, 0:I], ACT.Silu).then_inc(g_silu, 1)
                act.wait_ge(ht_mm, g * UNROLL + k + 2)
                act.activation(ht_sb[:, (k + 1) % 2, :], pk[4 + (k + 1) % 2][0:IC, 0:2 * P], ACT.Copy).then_inc(ht_ev, 1)
                act.wait_ge(y_mm, g * UNROLL + k + 1)
                act.wait_ge(w_rdy, g * UNROLL + k + 1)
                if k < 2:
                    act.wait_ge(sc_done[k % 2], g * (8 * UNROLL) + 16)
                else:
                    act.wait_ge(sc_done[k % 2], g * (8 * UNROLL) + 32)
                act.activation(y_sb[:, k % 2, :], pk[6 + k % 2][:, 0:H], ACT.Copy, scale=wslot[:, k:k + 1]).then_inc(y_ev, 1)


            def last_two(k):
                act.wait_ge(ht_mm, full + 2)
                act.activation(ht_sb[:, (k + 1) % 2, :], pk[4 + (k + 1) % 2][0:IC, 0:2 * P], ACT.Copy).then_inc(ht_ev, 1)
                for i in range(2):
                    a, u = (k + i) % 2, (k + i) % UNROLL
                    act.wait_ge(y_mm, full + (1 + i))
                    act.wait_ge(w_rdy, full + (1 + i))
                    act.wait_ge(sc_done[a], ((full + (2 + i)) >> 1) * 16)
                    act.activation(y_sb[:, a, :], pk[6 + a][:, 0:H], ACT.Copy, scale=wslot[:, u:u + 1]).then_inc(y_ev, 1)

            with act.Fori(0, GROUPS) as g:
                with act.If(g * UNROLL < full):
                    slot(g, 0)
                    with act.If(g * UNROLL + 1 < full):
                        slot(g, 1)
                        with act.If(g * UNROLL + 2 < full):
                            slot(g, 2)
                            with act.If(g * UNROLL + 3 < full):
                                slot(g, 3)
                            with act.Else():
                                last_two(3)
                        with act.Else():
                            last_two(2)
                    with act.Else():
                        last_two(1)
                with act.Else():
                    with act.If(g * UNROLL == full):
                        last_two(0)
        @block.vector
        def _(dve):
            for j in range(NJ):
                if j % (NJ // 2) == 0:
                    dve.wait_ge(l_x[j // (NJ // 2)], 16)
                last = dve.bn_stats(st1[:, j, :], x_sb[:, j, :])
            last.then_inc(dve_ch, 1)
            dve.wait_ge(dve_ch, 1)
            for j in range(NJ):
                last = dve.bn_aggr(mv1[:, j, :], st1[:, j, :])
            last.then_inc(st1_rdy, 1)
            chain = [1]
            count = [0] * 5

            def link(ins):
                chain[0] += 1
                ins.then_inc(dve_ch, 1)
                dve.wait_ge(dve_ch, chain[0])

            def step(i, make):
                if count[i]:
                    dve.wait_ge(chain_k[i], count[i])
                count[i] += 1
                make().then_inc(chain_k[i], 1)

            def x1(b):
                dve.wait_ge(at_mm, b + 1)
                dve.wait_ge(xa_rdy, 2 * b + 2)
                dve.wait_ge(c_pool, 16)
                for i in range(2):
                    j = 2 * b + i
                    last = dve.tensor_tensor(out=x_sb[:, j, :], in0=pk[3][:, i * N:(i + 1) * N], in1=x_sb[:, j, :], op=ALU.add)
                chain[0] += 1
                last.then_inc(dve_ch, 1)
                dve.wait_ge(dve_ch, chain[0])
                if b:
                    dve.wait_ge(xn_rdy, 2 * b)
                for i in range(2):
                    last = dve.bn_stats(st2[:, i, :], x_sb[:, 2 * b + i, :])
                link(last)
                for i in range(2):
                    last = dve.bn_aggr(mv2[:, i, :], st2[:, i, :])
                last.then_inc(st2_rdy, 1)

            def router(b):
                dve.wait_ge(lg_mm, 2 * b + 2)
                for i in range(2):
                    last = dve.max(v8[:, 2 * b + i, :], pk[5][:, i * E:(i + 1) * E])
                link(last)
                for i in range(2):
                    last = dve.max_index(i8[:, 2 * b + i, :], v8[:, 2 * b + i, :], pk[5][:, i * E:(i + 1) * E])
                last.then_inc(lg_ev, 1)

            full = (KTH - 1) // 8
            for b in range(NB):
                for r in range(full + 1):
                    for i in range(2):
                        if r == 0:
                            dve.wait_ge(sim_ev, 2 * b + i + 1)
                            if b:
                                dve.wait_ge(masked, 2 * b - 1 + i)
                            src = s_sb[b % 2][:, i, :]
                        else:
                            src = work_sb[:, i, :]
                        step(i, lambda: dve.max(m8[:, i, :], src))
                    if r < full:
                        for i in range(2):
                            src = s_sb[b % 2][:, i, :] if r == 0 else work_sb[:, i, :]
                            step(i, lambda: dve.match_replace(out=work_sb[:, i, :], in_to_replace=m8[:, i, :],
                                                              in_values=src, imm_value=NEG))
                    if b and r == 3:
                        x1(b - 1)
                    if b and r == 9:
                        router(b - 1)
                kth = (KTH - 1) % 8
                for i in range(2):
                    dve.wait_ge(chain_k[i], count[i])
                    dve.wait_ge(sig_rdy, 2 * b + i + 1)
                    if b:
                        dve.wait_ge(at_mm, b)
                        dve.wait_ge(xa_rdy, 2 * b)
                    dve.scalar_tensor_tensor(out=a_sb[:, i, :], in0=s_sb[b % 2][:, i, :], scalar=m8[:, i, kth:kth + 1],
                                             in1=sig_sb[:, i, :], op0=ALU.is_ge, op1=ALU.mult).then_inc(masked, 1)
            def one_hots(j0, j1):
                n = j1 - j0
                link(dve.tensor_copy(idx_f[:, j0:j1, :], i8[:, j0:j1, 0:TOPK]))
                iota_b = iota_f[:, 0:E].rearrange("p (j k e) -> p j k e", j=1, k=1).to_broadcast([P, n, TOPK, E])
                idx_b = idx_f[:, j0:j1, :].rearrange("p j (k o) -> p j k o", o=1).to_broadcast([P, n, TOPK, E])
                dve.tensor_tensor(out=onehot[:, j0 * TOPK:j1 * TOPK, :].rearrange("p (j k) e -> p j k e", k=TOPK), in0=iota_b, in1=idx_b,
                                  op=ALU.is_equal).then_inc(oh_rdy, 1)

            def rank_products(j0, j1, rank_ps):
                rank_b = rank_ps.rearrange("p (j o e) -> p j o e", o=1, e=E).to_broadcast([P, j1 - j0, TOPK, E])
                oh = onehot[:, j0 * TOPK:j1 * TOPK, :].rearrange("p (j k) e -> p j k e", k=TOPK)
                return dve.tensor_tensor(out=prod[:, j0 * TOPK:j1 * TOPK, :].rearrange("p (j k) e -> p j k e", k=TOPK),
                                         in0=oh, in1=rank_b, op=ALU.mult)

            def rank_sums(c0, c1):
                return dve.reduce_sum(sl_f[:, c0:c1], prod[:, c0:c1, :], axis=AX)

            def rank_integers(c0, c1):
                return dve.tensor_copy(sl_i[:, 0, c0:c1], sl_f[:, c0:c1])

            def rank_parts(c0, c1):
                dve.tensor_scalar(sl_i[:, 1, c0:c1], sl_i[:, 0, c0:c1], P - 1, None, ALU.bitwise_and)
                return dve.tensor_scalar(sl_i[:, 2, c0:c1], sl_i[:, 0, c0:c1], 7, None, ALU.logical_shift_right)

            def rank_floats(c0, c1):
                return dve.tensor_copy(sl_p[:, :, c0:c1], sl_i[:, 1:3, c0:c1])

            def slot_one_hots(c0, c1):
                for c in range(c0, c1):
                    if c < EARLY * TOPK:
                        last = dve.tensor_scalar(slot_oh[:, c, :], iota_h[:, :], sl_p[:, 0, c:c + 1], None, ALU.is_equal)
                    else:
                        last = dve.tensor_scalar(slot_oh[:, c, :], iota_h[:, :], sl_p[:, 0, c:c + 1], tok1[:, c // TOPK:c // TOPK + 1],
                                                 ALU.is_equal, ALU.mult)
                    if c % TOPK == TOPK - 1:
                        last.then_inc(soh_rdy, 1)

            dve.wait_ge(lg_ev, NB - 1)
            one_hots(0, EARLY)
            dve.wait_ge(masked, 2 * NB)
            x1(NB - 1)
            dve.wait_ge(rank_mm, 1)
            link(rank_products(0, EARLY, pk[1][:, 0:EARLY * E]))
            link(rank_sums(0, EARLY * TOPK))
            link(rank_integers(0, EARLY * TOPK))
            link(rank_parts(0, EARLY * TOPK))
            link(rank_floats(0, EARLY * TOPK))
            slot_one_hots(0, 16)
            router(NB - 1)
            dve.wait_ge(lg_ev, NB)
            one_hots(EARLY, NJ)
            dve.tensor_tensor(out=ex[:, :, :], in0=v8[:, :, 0:TOPK], in1=v8[:, :, 0:1].to_broadcast([P, NJ, TOPK]),
                              op=ALU.subtract).then_inc(v_rdy, 1)
            slot_one_hots(16, EARLY * TOPK)
            dve.wait_ge(rank_mm, 2)
            late_ps = pk[2][:, 0:(NJ - EARLY + 1) * E]
            c0, c1 = EARLY * TOPK, NJ * TOPK
            step(2, lambda: dve.tensor_scalar(cnt_i[:, 0, :], late_ps[:, (NJ - EARLY) * E:], float(P - 1), None, ALU.add))
            step(3, lambda: rank_products(EARLY, NJ, late_ps[:, 0:(NJ - EARLY) * E]))
            step(2, lambda: dve.tensor_scalar(cnt_i[:, 1, :], cnt_i[:, 0, :], 7, None, ALU.logical_shift_right))
            step(3, lambda: rank_sums(c0, c1))
            step(2, lambda: dve.tensor_copy(ntl[:, 0, :], cnt_i[:, 1, :]))
            step(3, lambda: rank_integers(c0, c1))
            step(2, lambda: dve.tensor_tensor_scan(ntl[:, 1, :], ones_f[:, 0:E], ntl[:, 0, :], 0.0, ALU.mult, ALU.add))
            step(3, lambda: rank_parts(c0, c1))
            step(2, lambda: dve.tensor_tensor(out=first_h, in0=ntl[:, 1, :], in1=ntl[:, 0, :], op=ALU.subtract))
            first_b = first_h.rearrange("p (o e) -> p o e", o=1).to_broadcast([P, NJ * TOPK, E])
            step(2, lambda: dve.tensor_tensor(out=prod_h, in0=onehot, in1=first_b, op=ALU.mult))
            step(3, lambda: rank_floats(c0, c1))
            step(2, lambda: dve.reduce_sum(sl_f[:, :], prod_h, axis=AX))
            dve.wait_ge(ex_rdy, 1)
            step(4, lambda: dve.reduce_sum(sm[:, 0, :], ex[:, :, :], axis=AX))
            dve.wait_ge(chain_k[3], count[3])
            step(2, lambda: dve.tensor_tensor(out=sl_t[:, :], in0=sl_p[:, 1, :], in1=sl_f[:, :], op=ALU.add))
            step(4, lambda: dve.reciprocal(sm[:, 1, :], sm[:, 0, :]))
            slot_one_hots(EARLY * TOPK, EARLY * TOPK + TOPK)
            step(4, lambda: dve.tensor_scalar(sm[:, 2, :], sm[:, 1, :], ROUTE_SCALE, None, ALU.mult))
            slot_one_hots(EARLY * TOPK + TOPK, NJ * TOPK)
            dve.wait_ge(chain_k[4], count[4])
            dve.tensor_tensor(out=rw, in0=ex[:, :, :], in1=sm[:, 2, :].rearrange("p (j o) -> p j o", o=1).to_broadcast([P, NJ, TOPK]),
                              op=ALU.mult).then_inc(rw_rdy, 1)
            dve.wait_ge(chain_k[2], count[2])
            dve.wait_ge(c_pool, 17)
            for q in range(NJ * TOPK // OHG):
                tile_b = sl_t[:, q * OHG:(q + 1) * OHG].rearrange("p (o c) -> p o c", o=1).to_broadcast([P, NCOL, OHG])
                dve.tensor_tensor(out=tile_oh[:, q, :, :], in0=iota_rep[:, :, :], in1=tile_b, op=ALU.is_equal).then_inc(toh_rdy, 1)
            link(dve.tensor_scalar(srank[:, 0, :], ntl[:, 1, :], pidx[:, 0:1], 0.0, ALU.is_le, ALU.add, accum_out=ecol[:, :]))
            dve.tensor_scalar(ediag[:, :], ident[:, 0:NCOL], ecol[:, 0:1], None, ALU.mult).then_inc(ed_rdy, 1)
            dve.tensor_scalar(full_i[:, :], ntl[:, 1, E - 1:E], -2.0, None, ALU.add)
            dve.wait_ge(tab_mm, 1)
            link(dve.tensor_scalar(tmp_t[:, :], pk[3][:, 0:NCOL], 0.0, pad_row[:, 0:1], ALU.is_equal, ALU.mult))
            dve.scalar_tensor_tensor(out=slot_row[:, :], in0=pk[3][:, 0:NCOL], scalar=-1.0, in1=tmp_t[:, :],
                                     op0=ALU.add, op1=ALU.add).then_inc(slots_rdy, 1)
            dve.wait_ge(et_mm, 1)
            dve.tensor_copy(etile[:, :], pk[5][:, 0:NCOL])
            link(dve.tensor_scalar(elow[:, :], pk[5][:, 0:NCOL], float(E - 1), None, ALU.min))
            dve.scalar_tensor_tensor(out=etwo_i[:, :], in0=elow[:, 0:NCOL - 2], scalar=float(E), in1=elow[:, 2:NCOL],
                                     op0=ALU.mult, op1=ALU.add).then_inc(tab_rdy, 1)

            def weights_of(expert_col, u):
                dve.scalar_tensor_tensor(out=srank[:, u, 0:TOPK], in0=xg_sb[:, u, H:H + TOPK], scalar=expert_col,
                                         in1=xg_sb[:, u, H + TOPK:XW], op0=ALU.is_equal, op1=ALU.mult,
                                         accum_out=wslot[:, u:u + 1]).then_inc(w_rdy, 1)

            def rows_out(k):
                dve.tensor_copy(xt_sb[:, k % 2, :], pk[k % 2][:, 0:KH * P]).then_inc(t_ev, 1)

            def gated(k):
                dve.tensor_tensor(out=h_sb[:, k % 2, :], in0=pk[2 + k % 2][:, I:GU], in1=sg_sb[:, k % 2, :],
                                  op=ALU.mult).then_inc(h_rdy, 1)

            dve.wait_ge(tab_rdy, 1)
            dve.wait_ge(sgu_mm, 2 * NB)
            dve.wait_ge(sht_mm, 2 * NB)
            full = dve.value_load(full_i[0:1, 0:1], min_val=MIN_TILES - 2, max_val=MAX_TILES - 2)
            for t in range(3):
                dve.wait_ge(t_mm, t + 1)
                rows_out(t)
                if t:
                    dve.wait_ge(g_silu, t)
                    gated(t - 1)
                dve.wait_ge(g_done[t], 16)
                weights_of(etile[:, t:t + 1], t)

            def slot(g, k):
                u = (k + 3) % UNROLL
                dve.wait_ge(t_mm, g * UNROLL + k + 4)
                rows_out(k + 1)
                dve.wait_ge(g_silu, g * UNROLL + k + 3)
                dve.wait_ge(ht_mm, g * UNROLL + k + 1)
                gated(k)
                dve.wait_ge(g_done[u], g * 16 + 16 * ((k + 3) // UNROLL + 1))
                dve.wait_ge(y_ev, g * UNROLL + k + 1)
                weights_of(etile[:, bass.ds(g * UNROLL + k + 3, 1)], u)

            with dve.Fori(0, GROUPS) as g:
                with dve.If(g * UNROLL < full):
                    slot(g, 0)
                    with dve.If(g * UNROLL + 1 < full):
                        slot(g, 1)
                        with dve.If(g * UNROLL + 2 < full):
                            slot(g, 2)
                            with dve.If(g * UNROLL + 3 < full):
                                slot(g, 3)
            for c in range(len(FINAL[0])):
                dve.wait_ge(f_ld[0][c], 16)
            for c, (j0, j1) in enumerate(FINAL[1]):
                dve.wait_ge(f_ld[1][c], 16)
                dve.tensor_tensor(out=fin[:, 0, j0:j1, :], in0=fin[:, 0, j0:j1, :], in1=fin[:, 1, j0:j1, :],
                                  op=ALU.add).then_inc(f_add, 1)

        @block.tensor
        def _(pe):
            pe.wait_ge(l_ctx, 16)

            def qk(b):
                for m in range(2):
                    pe.matmul(pk[4 + b][0:DC, m * N:(m + 1) * N], wqk_sb[:, m * DC:(m + 1) * DC], ctx_sb[:, b * N:(b + 1) * N],
                              start=True, stop=True).then_inc(qk_mm, 1)

            def sims(b):
                pe.wait_ge(qk_ev, 2 * b + 2)
                for i in range(2):
                    if b:
                        pe.wait_ge(sig_ev, 2 * b - 1 + i)
                    r0 = (2 * b + i) * P
                    pe.matmul(pk[1 + i][:, 0:N], qt_sb[:, r0:r0 + P], kt_sb[:, b * N:(b + 1) * N],
                              start=True, stop=True).then_inc(sim_mm, 1)

            def shared_out(b):
                for i in range(2):
                    pe.wait_ge(sh_rdy, 2 * b + i + 1)
                    pe.wait_ge(sgu_ev, 2 * b + i + 1)
                    for c in range(2):
                        last = pe.transpose(pk[6 + i][0:IC, c * P:(c + 1) * P], h_sb[:, i, c * IC:(c + 1) * IC], ident[:, :])
                    last.then_inc(sht_mm, 1)
                for i in range(2):
                    n = 2 * b + i
                    pe.wait_ge(sht_ev, n + 1)
                    for c in range(2):
                        last = pe.matmul(pk[6 + i][:, 2 * P:2 * P + H], ht_sb[:, i, c * P:(c + 1) * P], wsd_sb[:, c * H:(c + 1) * H],
                                         start=c == 0, stop=c == 1)
                    last.then_inc(sy_mm, 1)

            oh = onehot.rearrange("p (j k) e -> p j k e", k=TOPK)

            def ranks_early():
                pe.wait_ge(oh_rdy, 1)
                pe.wait_ge(sig_ev, 2 * NB)
                for k in range(TOPK):
                    pe.matmul(pk[1][:, 0:EARLY * E], before_h[:, :], oh[:, 0:EARLY, k, :], start=k == 0, stop=False, skip_group_check=True)
                for j in range(EARLY - 1):
                    for k in range(TOPK):
                        last = pe.matmul(pk[1][:, (j + 1) * E:EARLY * E].rearrange("p (m e) -> p m e", e=E), ones_h[:, :],
                                         oh[:, j:j + 1, k, :].to_broadcast([P, EARLY - 1 - j, E]), start=False,
                                         stop=(j == EARLY - 2 and k == TOPK - 1), skip_group_check=True)
                last.then_inc(rank_mm, 1)
                for j in range(EARLY):
                    for k in range(TOPK):
                        pe.matmul(pk[2][:, 0:(NJ - EARLY + 1) * E].rearrange("p (m e) -> p m e", e=E), ones_h[:, :],
                                  oh[:, j:j + 1, k, :].to_broadcast([P, NJ - EARLY + 1, E]), start=(j == 0 and k == 0), stop=False,
                                  skip_group_check=True)

            def ranks_late():
                pe.wait_ge(oh_rdy, 2)
                late = NJ - EARLY
                for k in range(TOPK):
                    pe.matmul(pk[2][:, 0:late * E], before_h[:, :], oh[:, EARLY:NJ, k, :], start=False, stop=False, skip_group_check=True)
                for j in range(late):
                    for k in range(TOPK):
                        last = pe.matmul(pk[2][:, (j + 1) * E:(late + 1) * E].rearrange("p (m e) -> p m e", e=E), ones_h[:, :],
                                         oh[:, EARLY + j:EARLY + j + 1, k, :].to_broadcast([P, late - j, E]), start=False,
                                         stop=(j == late - 1 and k == TOPK - 1), skip_group_check=True)
                last.then_inc(rank_mm, 1)

            def transpose_a(b):
                pe.wait_ge(masked, 2 * b + 2)
                if b:
                    pe.wait_ge(st2_rdy, b)
                for i in range(2):
                    for c in range(2):
                        last = pe.transpose(pk[3][:, i * N + c * P:i * N + (c + 1) * P], a_sb[:, c, i * P:(i + 1) * P], ident[:, :])
                last.then_inc(at_mm, 1)

            qk(0)
            sims(0)
            qk(1)
            sims(1)
            qk(2)
            qk(3)
            pe.wait_ge(c_pool, 16)
            transpose_a(0)
            for b in range(NB):
                if b + 2 < NB:
                    sims(b + 2)
                if b == NB - 1:
                    ranks_early()
                if b:
                    shared_out(b - 1)
                for i in range(2):
                    n = 2 * b + i
                    pe.wait_ge(xn_rdy, n + 1)
                    if b:
                        pe.wait_ge(xnt_ev, n - 1)
                    for c in range(KH):
                        last = pe.transpose(xnt_ps[i][:, c * P:(c + 1) * P], xn_of[b % 2][:, i, c * P:(c + 1) * P], ident[:, :])
                    last.then_inc(xnt_mm, 1)
                if b:
                    pe.wait_ge(lg_ev, b)
                pe.wait_ge(l_rt, 32)
                for i in range(2):
                    pe.matmul(pk[5][:, i * E:(i + 1) * E], ones_f[0:1, :], rb_sb[:, :], start=True, stop=False)
                    pe.wait_ge(xnt_ev, 2 * b + i + 1)
                    for c in range(KH):
                        last = pe.matmul(pk[5][:, i * E:(i + 1) * E], xt_sb[:, i, c * P:(c + 1) * P], rw_sb[:, c * E:(c + 1) * E],
                                         start=False, stop=c == KH - 1)
                    last.then_inc(lg_mm, 1)
                pe.wait_ge(l_ws, 32)
                for i in range(2):
                    n = 2 * b + i
                    if i and b + 1 < NB:
                        transpose_a(b + 1)
                    if n == NJ - 1:
                        ranks_late()
                    if b:
                        pe.wait_ge(sy_ev, n - 1)
                    for c in range(KH):
                        last = pe.matmul(pk[6 + i][:, 0:GU], xt_sb[:, i, c * P:(c + 1) * P], wsgu_sb[:, c * GU:(c + 1) * GU],
                                         start=c == 0, stop=c == KH - 1)
                    last.then_inc(sgu_mm, 1)
            shared_out(NB - 1)
            for c in range(NJ * TOPK):
                if c % OHG == 0:
                    if c < EARLY * TOPK:
                        pe.wait_ge(tok_rdy, (c + OHG) // TOPK)
                    else:
                        pe.wait_ge(soh_rdy, NJ)
                    pe.wait_ge(toh_rdy, c // OHG + 1)
                last = pe.matmul(pk[3][:, 0:NCOL], slot_oh[:, c, :], tile_oh[:, c // OHG, :, c % OHG], start=c == 0, stop=c == NJ * TOPK - 1)
            last.then_inc(tab_mm, 1)
            pe.wait_ge(ed_rdy, 1)
            pe.matmul(pk[5][:, 0:NCOL], ones_h[:, :], ediag[:, :], start=True, stop=True).then_inc(et_mm, 1)
            for _ in range(3):
                pe.matmul(pk[4][:, :], ident[:, :], wsgu_sb[:, 0:512], start=True, stop=True)
            for s in l_w:
                pe.wait_ge(s, 16)

            def rows_t(k, u):
                for c in range(KH):
                    last = pe.transpose(pk[k % 2][:, c * P:(c + 1) * P], xg_sb[:, u, c * P:(c + 1) * P], ident[:, :])
                last.then_inc(t_mm, 1)

            def gate_up(k, e):
                for c in range(KH):
                    last = pe.matmul(pk[2 + k % 2][:, 0:GU], xt_sb[:, k % 2, c * P:(c + 1) * P],
                                     wgu_sb[:, bass.ds(e, 1), c * GU:(c + 1) * GU], start=c == 0, stop=c == KH - 1)
                last.then_inc(g_mm, 1)

            def h_t(k):
                for c in range(2):
                    last = pe.transpose(pk[4 + k % 2][0:IC, c * P:(c + 1) * P], h_sb[:, k % 2, c * IC:(c + 1) * IC], ident[:, :])
                last.then_inc(ht_mm, 1)

            def down(k, e):
                for c in range(2):
                    last = pe.matmul(pk[6 + k % 2][:, 0:H], ht_sb[:, k % 2, c * P:(c + 1) * P],
                                     wd_sb[:, bass.ds(e, 1), c * H:(c + 1) * H], start=c == 0, stop=c == 1)
                last.then_inc(y_mm, 1)

            def experts(t):
                two = pe.value_load(etwo_i[0:1, t:t + 1] if isinstance(t, int) else etwo_i[0:1, bass.ds(t, 1)], min_val=0, max_val=E * E - 1)
                return (two >> 5) & (E - 1), two & (E - 1)

            pe.wait_ge(tab_rdy, 1)
            pe.wait_ge(sy_ev, 2 * NB)
            full = pe.value_load(full_i[0:1, 0:1], min_val=MIN_TILES - 2, max_val=MAX_TILES - 2)
            e_first = [experts(t)[0] for t in range(2)]
            pe.wait_ge(g_done[0], 16)
            rows_t(0, 0)
            for t in range(2):
                e_up = e_first[t]
                pe.wait_ge(t_ev, t + 1)
                gate_up(t, e_up)
                pe.wait_ge(g_done[t + 1], 16)
                rows_t(t + 1, t + 1)
            pe.wait_ge(h_rdy, 1)
            h_t(0)

            def slot(g, k):
                u = (k + 3) % UNROLL
                if k == 0:
                    of[0], of[2] = experts(g * UNROLL)
                pe.wait_ge(t_ev, g * UNROLL + k + 3)
                pe.wait_ge(h_rdy, g * UNROLL + k + 1)
                gate_up(k, of[k + 2])
                if k == 0:
                    of[1], of[3] = experts(g * UNROLL + 1)
                elif k < UNROLL - 1:
                    of[k + 3] = experts(g * UNROLL + k + 1)[1]
                pe.wait_ge(g_done[u], g * 16 + 16 * ((k + 3) // UNROLL + 1))
                rows_t(k + 1, u)
                pe.wait_ge(h_rdy, g * UNROLL + k + 2)
                pe.wait_ge(ht_ev, g * UNROLL + max(k, 1))
                h_t(k + 1)
                pe.wait_ge(ht_ev, g * UNROLL + k + 1)
                pe.wait_ge(y_ev, g * UNROLL + max(k, 1))
                down(k, of[k])

            def last_two(k):
                if k == 0:
                    of[0], of[1] = experts(full)[0], experts(full + 1)[0]
                pe.wait_ge(h_rdy, full + 2)
                pe.wait_ge(ht_ev, full)
                h_t(k + 1)
                for i in range(2):
                    pe.wait_ge(ht_ev, full + (1 + i))
                    pe.wait_ge(y_ev, full + i)
                    down(k + i, of[k + i])

            of = {}
            with pe.Fori(0, GROUPS) as g:
                with pe.If(g * UNROLL < full):
                    slot(g, 0)
                    with pe.If(g * UNROLL + 1 < full):
                        slot(g, 1)
                        with pe.If(g * UNROLL + 2 < full):
                            slot(g, 2)
                            with pe.If(g * UNROLL + 3 < full):
                                slot(g, 3)
                            with pe.Else():
                                last_two(3)
                        with pe.Else():
                            last_two(2)
                    with pe.Else():
                        last_two(1)
                with pe.Else():
                    with pe.If(g * UNROLL == full):
                        last_two(0)


def kernel(x, ctx_512, L0_xattn_Wq, L0_xattn_Wk, L0_xattn_gamma_raw, L0_ffn_router_w, L0_ffn_router_b,
           L0_ffn_gate_w, L0_ffn_up_w, L0_ffn_down_w, L0_ffn_shared_gate_w, L0_ffn_shared_up_w, L0_ffn_shared_down_w):
    import numpy as np
    import concourse.bacc as bacc
    from concourse import mybir as mb
    from concourse.bass_utils import run_bass_kernel_spmd

    def chunks(w, k):
        return np.ascontiguousarray(w.T.reshape(-1, k, w.shape[0]).transpose(1, 0, 2).reshape(k, -1))

    gu = np.concatenate([np.asarray(L0_ffn_gate_w), np.asarray(L0_ffn_up_w)], axis=1)
    gu = gu.transpose(2, 0, 1).reshape(KH, P, E, GU).transpose(1, 2, 0, 3).reshape(P, E, KH * GU)
    dn = np.asarray(L0_ffn_down_w).transpose(2, 0, 1).reshape(2, IC, E, H).transpose(1, 2, 0, 3).reshape(IC, E, 2 * H)
    arrays = {
        "x_dram": np.asarray(x).reshape(TOK, H),
        "ctx_wqk_dram": np.concatenate([np.asarray(ctx_512).reshape(TOK, DC).T, np.asarray(L0_xattn_Wq).T,
                                        np.asarray(L0_xattn_Wk).T], axis=1),
        "gamma_dram": np.asarray(L0_xattn_gamma_raw).reshape(1, 1),
        "router_w_dram": chunks(np.asarray(L0_ffn_router_w), P),
        "router_b_dram": np.asarray(L0_ffn_router_b).reshape(1, E),
        "w_gu_dram": gu,
        "w_down_dram": dn,
        "ws_gu_dram": chunks(np.concatenate([np.asarray(L0_ffn_shared_gate_w), np.asarray(L0_ffn_shared_up_w)], axis=0), P),
        "ws_down_dram": chunks(np.asarray(L0_ffn_shared_down_w), IC),
    }
    arrays = {n: np.ascontiguousarray(a) for n, a in arrays.items()}
    nc = bacc.Bacc("TRN2", target_bir_lowering=False, num_devices=1, dynamic_dma_scratch_size=8192)
    args = [nc.dram_tensor(n, a.shape, mb.dt.from_np(a.dtype), kind="ExternalInput").ap() for n, a in arrays.items()]
    out = nc.dram_tensor("out_dram", (TOK, H), mb.dt.float32, kind="ExternalOutput").ap()
    build(nc, *args, out)
    r = run_bass_kernel_spmd(nc, [arrays], core_ids=[0])
    return r.results[0]["out_dram"].reshape(NB, N, H)
```
